# Optimizing a Trainium2 kernel written in Bass

```python
import numpy as np
import jax
import jax.numpy as jnp

def _softmax(x, axis=-1):
    return jax.nn.softmax(x, axis=axis)

def _gelu(x):
    return jax.nn.gelu(x, approximate=True)

def _silu(x):
    return jax.nn.silu(x)

def _sigmoid(x):
    return jax.nn.sigmoid(x)

def _layernorm(x, axis=-1, eps=1e-05):
    m = jnp.mean(x, axis=axis, keepdims=True)
    v = jnp.var(x, axis=axis, keepdims=True)
    return (x - m) / jnp.sqrt(v + eps)

def _scatter_add(tgt, idx, src, axis=0):
    return tgt.at[idx].add(src)

def _segment_sum(src, seg, n):
    return jax.ops.segment_sum(src, seg, n)
kernel_name = 'mk_seq_preln_d2_jaxref_r8_7256ff'

def setup_inputs(seed: int=0):
    np.random.seed(seed)
    _w = jnp.asarray

    def _L0_attn_setup():
        import jax, jax.numpy as jnp
        import numpy as np
        HEADS = 16
        DIMS = [64, 64, 64, 64]
        EPS = 0.0001
        P_POW = 2

        def _cdist(Q, K):
            q2 = jnp.sum(Q * Q, axis=-1)
            k2 = jnp.sum(K * K, axis=-1)
            qk = jnp.einsum('hbtd,hbsd->hbts', Q, K)
            d2 = q2[..., :, None] + k2[..., None, :] - 2.0 * qk
            return jnp.sqrt(jnp.maximum(d2, 0.0))
        key = jax.random.key(seed)
        ks = jax.random.split(key, 4)
        b, t, d_in = (2, 256, 128)
        d_proj = HEADS * sum(DIMS)
        X = jax.random.normal(ks[0], (b, t, d_in), dtype=jnp.float32)
        W_in = jax.random.normal(ks[1], (d_in, d_proj), dtype=jnp.float32) * d_in ** (-0.5)
        b_in = jnp.zeros((d_proj,), dtype=jnp.float32)
        W_out = jax.random.normal(ks[2], (HEADS * DIMS[2], d_in), dtype=jnp.float32) * (HEADS * DIMS[2]) ** (-0.5)
        b_out = jnp.zeros((d_in,), dtype=jnp.float32)
        return {'X': X, 'W_in': W_in, 'b_in': b_in, 'W_out': W_out, 'b_out': b_out}
    _L0_attn_in = _L0_attn_setup()

    def _L0_ffn_setup():
        import jax, jax.numpy as jnp
        import numpy as np
        B, S, D = (4, 256, 128)
        EXP = 4
        H = EXP * D
        E = 8
        TOP_K = 2
        key = jax.random.key(seed)
        ks = jax.random.split(key, 8)
        scale1 = 1.0 / np.sqrt(D)
        scale2 = 1.0 / np.sqrt(H)
        x = jax.random.normal(ks[0], (B, S, D), dtype=jnp.float32)
        W1 = jax.random.uniform(ks[1], (E, D, H), jnp.float32, -scale1, scale1)
        b1 = jax.random.uniform(ks[2], (E, H), jnp.float32, -scale1, scale1)
        W2 = jax.random.uniform(ks[3], (E, H, D), jnp.float32, -scale2, scale2)
        b2 = jax.random.uniform(ks[4], (E, D), jnp.float32, -scale2, scale2)
        Wr = jax.random.uniform(ks[5], (D, E), jnp.float32, -scale1, scale1)
        br = jax.random.uniform(ks[6], (E,), jnp.float32, -scale1, scale1)
        return {'input_emb': x, 'W1': W1, 'b1': b1, 'W2': W2, 'b2': b2, 'Wr': Wr, 'br': br}
    _L0_ffn_in = _L0_ffn_setup()

    def _L1_attn_setup():
        import jax, jax.numpy as jnp
        import numpy as np
        EPS = 1e-06
        N_HEADS = 16

        def _heads(t, B, N, H, Dk):
            return t.reshape(B, N, H, Dk).transpose(0, 2, 1, 3)
        key = jax.random.key(seed)
        ks = jax.random.split(key, 5)
        B, N, D = (64, 64, 128)
        x = jax.random.normal(ks[0], (B, N, D), dtype=jnp.float32)
        s = 0.02
        W_q = jax.random.normal(ks[1], (D, D), dtype=jnp.float32) * s
        W_k = jax.random.normal(ks[2], (D, D), dtype=jnp.float32) * s
        W_v = jax.random.normal(ks[3], (D, D), dtype=jnp.float32) * s
        W_o = jax.random.normal(ks[4], (D, D), dtype=jnp.float32) * s
        z = jnp.zeros((D,), dtype=jnp.float32)
        return {'x': x, 'W_q': W_q, 'b_q': z, 'W_k': W_k, 'b_k': z, 'W_v': W_v, 'b_v': z, 'W_o': W_o, 'b_o': z}
    _L1_attn_in = _L1_attn_setup()

    def _L1_ffn_setup():
        import jax, jax.numpy as jnp
        import numpy as np
        CAPACITY_RATIO = 0.75
        key = jax.random.key(seed)
        k1, k2, k3 = jax.random.split(key, 3)
        B, L, D = (4, 1024, 128)
        x = jax.random.normal(k1, (B, L, D), dtype=jnp.float32)
        w_router = jax.random.normal(k2, (D,), dtype=jnp.float32) * 0.02
        w_block = jax.random.normal(k3, (D, D), dtype=jnp.float32) * 0.02
        return {'x': x, 'w_router': w_router, 'w_block': w_block}
    _L1_ffn_in = _L1_ffn_setup()
    _d = {'L0_attn_X': _L0_attn_in['X'], 'L0_attn_W_in': _L0_attn_in['W_in'], 'L0_attn_b_in': _L0_attn_in['b_in'], 'L0_attn_W_out': _L0_attn_in['W_out'], 'L0_attn_b_out': _L0_attn_in['b_out'], 'L0_ffn_W1': _L0_ffn_in['W1'], 'L0_ffn_b1': _L0_ffn_in['b1'], 'L0_ffn_W2': _L0_ffn_in['W2'], 'L0_ffn_b2': _L0_ffn_in['b2'], 'L0_ffn_Wr': _L0_ffn_in['Wr'], 'L0_ffn_br': _L0_ffn_in['br'], 'L1_attn_W_q': _L1_attn_in['W_q'], 'L1_attn_b_q': _L1_attn_in['b_q'], 'L1_attn_W_k': _L1_attn_in['W_k'], 'L1_attn_b_k': _L1_attn_in['b_k'], 'L1_attn_W_v': _L1_attn_in['W_v'], 'L1_attn_b_v': _L1_attn_in['b_v'], 'L1_attn_W_o': _L1_attn_in['W_o'], 'L1_attn_b_o': _L1_attn_in['b_o'], 'L1_ffn_w_router': _L1_ffn_in['w_router'], 'L1_ffn_w_block': _L1_ffn_in['w_block']}
    _x0 = _d['L0_attn_X']
    _d['L0_attn_X'] = jax.random.normal(jax.random.fold_in(jax.random.key(seed), 1), (8, 512, 128), dtype=_x0.dtype)
    del _x0
    return _d

def reference(L0_attn_X, L0_attn_W_in, L0_attn_b_in, L0_attn_W_out, L0_attn_b_out, L0_ffn_W1, L0_ffn_b1, L0_ffn_W2, L0_ffn_b2, L0_ffn_Wr, L0_ffn_br, L1_attn_W_q, L1_attn_b_q, L1_attn_W_k, L1_attn_b_k, L1_attn_W_v, L1_attn_b_v, L1_attn_W_o, L1_attn_b_o, L1_ffn_w_router, L1_ffn_w_block):

    def _L0_attn_ref(X, W_in, b_in, W_out, b_out):
        import jax, jax.numpy as jnp
        import numpy as np
        HEADS = 16
        DIMS = [64, 64, 64, 64]
        EPS = 0.0001
        P_POW = 2

        def _cdist(Q, K):
            q2 = jnp.sum(Q * Q, axis=-1)
            k2 = jnp.sum(K * K, axis=-1)
            qk = jnp.einsum('hbtd,hbsd->hbts', Q, K)
            d2 = q2[..., :, None] + k2[..., None, :] - 2.0 * qk
            return jnp.sqrt(jnp.maximum(d2, 0.0))
        b, t, _ = X.shape
        P = X @ W_in + b_in
        P = P.reshape(b, t, HEADS, sum(DIMS))
        P = jnp.transpose(P, (2, 0, 1, 3))
        splits = np.cumsum(DIMS)[:-1]
        Q, K, V, G = jnp.split(P, splits, axis=-1)
        W = jnp.power(EPS + _cdist(Q, K), -P_POW)
        W = W / (EPS + jnp.sum(W, axis=-1, keepdims=True))
        A = jnp.einsum('hbts,hbse->hbte', W, V)
        H = G * A
        H = jnp.transpose(H, (1, 2, 0, 3)).reshape(b, t, HEADS * DIMS[2])
        return H @ W_out + b_out

    def _L0_ffn_ref(input_emb, W1, b1, W2, b2, Wr, br):
        import jax, jax.numpy as jnp
        import numpy as np
        B, S, D = (4, 256, 128)
        EXP = 4
        H = EXP * D
        E = 8
        TOP_K = 2
        logits = jnp.einsum('bsd,de->bse', input_emb, Wr) + br
        route_w = jax.nn.softmax(logits, axis=-1)
        _, topk_idx = jax.lax.top_k(route_w, TOP_K)
        mask = jax.nn.one_hot(topk_idx, E, dtype=route_w.dtype).sum(-2)
        routed = route_w * mask
        routed = routed / routed.sum(axis=-1, keepdims=True)
        h = jax.nn.relu(jnp.einsum('bsd,edh->ebsh', input_emb, W1) + b1[:, None, None, :])
        expert_out = jnp.einsum('ebsh,ehd->ebsd', h, W2) + b2[:, None, None, :]
        return jnp.einsum('bse,ebsd->bsd', routed, expert_out)

    def _L1_attn_ref(x, W_q, b_q, W_k, b_k, W_v, b_v, W_o, b_o):
        import jax, jax.numpy as jnp
        import numpy as np
        EPS = 1e-06
        N_HEADS = 16

        def _heads(t, B, N, H, Dk):
            return t.reshape(B, N, H, Dk).transpose(0, 2, 1, 3)
        B, N, Dm = x.shape
        H = N_HEADS
        Dk = Dm // H
        q = _heads(x @ W_q.T + b_q, B, N, H, Dk)
        k = _heads(x @ W_k.T + b_k, B, N, H, Dk)
        v = _heads(x @ W_v.T + b_v, B, N, H, Dk)
        dec = jnp.exp(-jnp.arange(N, dtype=jnp.float32) / N)[None, None, :, None]
        qf = jax.nn.relu(q) * dec
        kf = jax.nn.relu(k) * dec
        KV = jnp.einsum('bhnd,bhne->bhde', kf, v)
        Ksum = kf.sum(axis=2)
        denom = jnp.einsum('bhnd,bhd->bhn', qf, Ksum) + EPS
        out = jnp.einsum('bhnd,bhde->bhne', qf, KV) / denom[..., None]
        out = out.transpose(0, 2, 1, 3).reshape(B, N, Dm)
        return out @ W_o.T + b_o

    def _L1_ffn_ref(x, w_router, w_block):
        import jax, jax.numpy as jnp
        import numpy as np
        CAPACITY_RATIO = 0.75
        B, L, D = x.shape
        k = max(1, int(L * CAPACITY_RATIO))
        scores = jnp.einsum('bld,d->bl', x, w_router)
        _, top_idx = jax.lax.top_k(scores, k)
        selected = jnp.take_along_axis(x, top_idx[:, :, None], axis=1)
        processed = jax.nn.gelu(jnp.einsum('bkd,de->bke', selected, w_block))
        batch_idx = jnp.arange(B)[:, None]
        out = x.at[batch_idx, top_idx].set(processed)
        return out
    x = L0_attn_X
    x = x + _L0_attn_ref(_layernorm(x, axis=-1), L0_attn_W_in, L0_attn_b_in, L0_attn_W_out, L0_attn_b_out)
    x = x + _L0_ffn_ref(_layernorm(x, axis=-1), L0_ffn_W1, L0_ffn_b1, L0_ffn_W2, L0_ffn_b2, L0_ffn_Wr, L0_ffn_br)
    x = x + _L1_attn_ref(_layernorm(x, axis=-1), L1_attn_W_q, L1_attn_b_q, L1_attn_W_k, L1_attn_b_k, L1_attn_W_v, L1_attn_b_v, L1_attn_W_o, L1_attn_b_o)
    x = x + _L1_ffn_ref(_layernorm(x, axis=-1), L1_ffn_w_router, L1_ffn_w_block)
    return x

_drawn_inputs = setup_inputs


def setup_inputs(seed=0):
    import zlib

    import numpy as np

    out = dict(_drawn_inputs(seed))
    spreads = {'L0_attn_b_in': (0.0, 0.1),
     'L0_attn_b_out': (0.0, 0.1),
     'L1_attn_b_q': (0.0, 0.482),
     'L1_attn_b_k': (0.0, 0.8),
     'L1_attn_b_v': (0.0, 0.284),
     'L1_attn_b_o': (0.0, 0.1)}
    factors = {'L1_attn_W_q': 3.341}
    for name, (base, spread) in spreads.items():
        noise = np.random.default_rng([zlib.crc32(name.encode()), seed]).standard_normal(out[name].shape)
        drawn = base * np.exp(spread * noise) if base else spread * noise
        out[name] = jnp.asarray(drawn.astype(out[name].dtype))
    for name, factor in factors.items():
        out[name] = (out[name] * factor).astype(out[name].dtype)
    return out
```

```python
from contextlib import ExitStack

import numpy as np

import concourse.bass as bass
from concourse import mybir

ALU = mybir.AluOpType
ACT = mybir.ActivationFunctionType
AX = mybir.AxisListType
F32 = mybir.dt.float32

P = 128
B, T, D = 8, 512, 128
NC = T // P
H0, E0 = 16, 64
PAIRS = H0 // 2
QUADS = H0 // 4
ATT_EPS = 1e-4
LN_EPS = 1e-5
NE, FF = 8, 512
NF = FF // P
TOP_K = 2
H1, E1 = 16, 8
LIN_EPS = 1e-6
KEEP = T * 3 // 4

N_V, N_QUAD, N_OUT = 2 * NC, 8, 2
N_BATCH = N_V + QUADS * N_QUAD + N_OUT


def build(nc, a, out):
    dsum = nc.dram_tensor("head_sums", (QUADS, 2, 2, T), F32, kind="Internal").ap()
    drec = nc.dram_tensor("head_recips", (QUADS, 2, 2, T), F32, kind="Internal").ap()
    with ExitStack() as ctx:
        x = ctx.enter_context(nc.sbuf_tensor("x", [P, B * NC, D], F32))
        ident = ctx.enter_context(nc.sbuf_tensor("ident", [P, P], F32))
        build_attention(nc, a, x, ident, dsum, drec)
        build_rest(nc, a, x, ident, out)


def build_attention(nc, a, x, ident, dsum, drec):
    with ExitStack() as ctx:
        def sb(name, shape):
            return ctx.enter_context(nc.sbuf_tensor(name, shape, F32))

        def psum(name, shape):
            return ctx.enter_context(nc.psum_tensor(name, shape, F32))

        def sem(name):
            return ctx.enter_context(nc.semaphore(name))

        xnT = sb("xnT", [P, B, T])
        xb = sb("xb", [P, T])
        wqkg = sb("wqkg", [P, PAIRS, 3, P])
        wv = sb("wv", [P, H0 * E0])
        wout = sb("wout", [P, PAIRS, D])
        bqkg = sb("bqkg", [P, PAIRS, 3])
        bv = sb("bv", [P, H0 * E0])
        bout = sb("bout", [P, 1])
        nsel = sb("nsel", [P, 2, P])
        holder = sb("holder", [P, 1])
        stats = sb("stats", [P, 2, NC, 6])
        mv = sb("mv", [P, 2, NC, 2])
        std = sb("std", [P, 2, NC])
        rstd = sb("rstd", [P, 2, NC])
        xn = sb("xn", [P, 2, NC, D])
        qk = sb("qk", [P, 2, T])
        sq = sb("sq", [P, 2, 2, T])
        query = sb("query", [P, 4, T])
        key = sb("key", [P, 4, T])
        gT = sb("gT", [P, PAIRS, T])
        hT = sb("hT", [P, PAIRS, T])
        vt = sb("vt", [P, NC, PAIRS, 3, E0])
        w = sb("w", [P, 4, NC, T])
        srow = sb("srow", [P, 2, T])
        ssum = sb("ssum", [P, 2 * 2 * T // P])
        srec = sb("srec", [P, 2 * 2 * T // P])
        oT = sb("oT", [P, T])

        pj = psum("pj", [P, 2, T])
        sc = psum("sc", [P, 2, 2, T])
        av = psum("av", [P, 2, T])

        s_in = sem("s_in")
        s_ones = sem("s_ones")
        s_stats = sem("s_stats")
        s_mv = sem("s_mv")
        s_std = sem("s_std")
        s_rstd = sem("s_rstd")
        s_xn = sem("s_xn")
        s_xnT_ps = sem("s_xnT_ps")
        s_xnT = sem("s_xnT")
        s_xb = sem("s_xb")
        s_pj = sem("s_pj")
        s_pj_free = sem("s_pj_free")
        s_sq = sem("s_sq")
        s_split = sem("s_split")
        s_sc = sem("s_sc")
        s_d2 = sem("s_d2")
        s_sqrt = sem("s_sqrt")
        s_ln = sem("s_ln")
        s_w = sem("s_w")
        s_av = sem("s_av")
        s_av_free = sem("s_av_free")
        s_srow = sem("s_srow")
        s_sum_out = sem("s_sum_out")
        s_sum_in = sem("s_sum_in")
        s_sume = sem("s_sume")
        s_rec = sem("s_rec")
        s_rec_out = sem("s_rec_out")
        s_bc = sem("s_bc")
        s_hT = sem("s_hT")

        N_IN = 9

        def head_base(b):
            return 0 if isinstance(b, int) and b == 0 else b * N_BATCH - N_OUT

        def quad_base(b, q):
            if isinstance(b, int) and b == 0:
                return N_V + q * N_QUAD
            return b * N_BATCH + (N_V + q * N_QUAD + (0 if q else -N_OUT))

        def out_base(b):
            if isinstance(b, int) and b == B - 1:
                return quad_base(b, QUADS - 1) + N_QUAD
            return quad_base(b + 1, 1) - N_OUT

        block = ctx.enter_context(nc.Block())

        @block.sync
        def _(sp):
            sp.dma_start(x[:, :, :], a["X"].rearrange("(n p) d -> p n d", p=P)).then_inc(s_in, 16)
            sp.dma_start(wqkg[:, :, :, :], a["W_qkg"]).then_inc(s_in, 16)
            sp.dma_start(wv[:, :], a["W_v"]).then_inc(s_in, 16)
            sp.dma_start(wout[:, :, :], a["W_out"].rearrange("(g p) d -> p g d", p=P)).then_inc(s_in, 16)
            sp.dma_start(bqkg[:, :, :], a["b_qkg"]).then_inc(s_in, 16)
            sp.dma_start(bv[:, :], a["b_v"].partition_broadcast(P)).then_inc(s_in, 16)
            sp.dma_start(bout[:, :], a["b_out"].rearrange("(p o) -> p o", o=1)).then_inc(s_in, 16)
            sp.dma_start(nsel[:, :, :], a["c_nsel"]).then_inc(s_in, 16)
            sp.dma_start(ident[:, :], a["c_ident"]).then_inc(s_in, 16)

            def normalizer(b, q):
                j = b * QUADS + q
                sp.wait_ge(s_srow, 4 * (j + 1))
                sp.dma_start(dsum[q:q + 1, :, 0, :], srow[64:65, :, :]).then_inc(s_sum_out, 16)
                sp.dma_start(dsum[q:q + 1, :, 1, :], srow[0:1, :, :]).then_inc(s_sum_out, 16)
                sp.wait_ge(s_sum_out, 32 * (j + 1))
                sp.dma_start(ssum[:, :], dsum[q].rearrange("g v t -> (g v t)").rearrange("(p k) -> p k", p=P)).then_inc(s_sum_in, 16)
                sp.wait_ge(s_rec, j + 1)
                sp.dma_start(drec[q].rearrange("g v t -> (g v t)").rearrange("(p k) -> p k", p=P), srec[:, :]).then_inc(s_rec_out, 16)
                sp.wait_ge(s_rec_out, 16 * (j + 1))
                for v in range(2):
                    sp.dma_start(hT[64 * v:64 * v + 64, 2 * q:2 * q + 2, :],
                                 drec[q, :, v, :].partition_broadcast(64)).then_inc(s_bc, 16)

            for q in range(QUADS - 1):
                normalizer(0, q)
            with sp.Fori(1, B) as b:
                normalizer(b - 1, QUADS - 1)
                sp.wait_ge(s_pj, out_base(b - 1) + 1)
                for q in range(QUADS - 1):
                    normalizer(b, q)
            normalizer(B - 1, QUADS - 1)

        @block.gpsimd
        def _(pool):
            nc.gpsimd.memset(query[:, :, :], 0.0).then_inc(s_ones, 1)
            nc.gpsimd.memset(key[:, :, :], 0.0).then_inc(s_ones, 1)
            nc.gpsimd.memset(vt[:, :, :, 1, :], 1.0).then_inc(s_ones, 1)
            pool.wait_ge(s_ones, 3)
            nc.gpsimd.memset(query[96:97, :, :], 1.0).then_inc(s_ones, 1)
            pool.wait_ge(s_ones, 4)
            nc.gpsimd.memset(key[64:65, :, :], 1.0).then_inc(s_ones, 1)
            pool.wait_ge(s_ones, 5)

            def copy_xb(b):
                pool.wait_ge(s_xnT, b + 1)
                if not isinstance(b, int):
                    pool.wait_ge(s_pj_free, quad_base(b - 1, 1))
                nc.gpsimd.tensor_copy(xb[:, :], xnT[:, bass.ds(b, 1), :].rearrange("p o t -> p (o t)")).then_inc(s_xb, 1)

            def squares(b, q):
                for r in range(2):
                    for i in range(2):
                        pool.wait_ge(s_pj_free, quad_base(b, q) + 3 * r + i + 1)
                        nc.gpsimd.tensor_tensor(sq[:, r, i, :], qk[:, i, :], qk[:, i, :], ALU.mult).then_inc(s_sq, 1)

            copy_xb(0)
            squares(0, 0)
            with pool.Fori(0, B - 1) as b:
                for q in range(1, QUADS):
                    squares(b, q)
                copy_xb(b + 1)
                squares(b + 1, 0)
            for q in range(1, QUADS):
                squares(B - 1, q)

        @block.tensor
        def _(pe):
            pe.wait_ge(s_in, 16 * N_IN)

            def turn(b, u):
                pe.wait_ge(s_xn, NC * (b + 1))
                if not isinstance(b, int):
                    pe.wait_ge(s_xnT, b - 1)
                for c in range(NC):
                    m = nc.tensor.transpose(pj[:, u, c * P:(c + 1) * P], xn[:, u, c, :], ident[:, :])
                m.then_inc(s_xnT_ps, 1)

            for u in range(2):
                turn(u, u)
            with pe.Fori(1, B // 2) as h:
                for u in range(2):
                    turn(2 * h + u, u)

            def bank_free(n):
                if not isinstance(n, int) or n >= 2:
                    pe.wait_ge(s_pj_free, n - 1)
                else:
                    pe.wait_ge(s_xnT, B)

            def values(b):
                pe.wait_ge(s_xb, b + 1)
                n = head_base(b)
                for c in range(NC):
                    for h in range(2):
                        bank_free(n + 2 * c + h)
                        nc.tensor.matmul(pj[:, h, :], xb[:, c * P:(c + 1) * P], wv[:, h * T:(h + 1) * T],
                                         start=True, stop=True).then_inc(s_pj, 1)

            def projections(b, q):
                n = quad_base(b, q)
                xT = xnT[:, bass.ds(b, 1), :].rearrange("p o t -> p (o t)")
                for r in range(2):
                    for i in range(3):
                        bank_free(n + 3 * r + i)
                        nc.tensor.matmul(pj[:, (3 * r + i) % 2, :], wqkg[:, 2 * q + r, i, :], xT,
                                         start=True, stop=True).then_inc(s_pj, 1)
                for r in range(2):
                    g = (b * QUADS + q) * 2 + r
                    bank_free(n + 6 + r)
                    pe.wait_ge(s_sq, 2 * g + 2)
                    nc.tensor.matmul(pj[:, r, :], nsel[:, 0, :], sq[:, r, 0, :], start=True, stop=False)
                    nc.tensor.matmul(pj[:, r, :], nsel[:, 1, :], sq[:, r, 1, :],
                                     start=False, stop=True).then_inc(s_pj, 1)

            def distances(b, q):
                for u in range(4):
                    n = (b * QUADS + q) * 4 + u
                    pe.wait_ge(s_pj_free, quad_base(b, q) + 7 + u // 2)
                    for h in range(2):
                        if not isinstance(n, int) or n >= 1:
                            pe.wait_ge(s_d2, 2 * n + h - 1)
                        for k in range(2):
                            c = 2 * h + k
                            m = nc.tensor.matmul(sc[:, h, k, :], key[:, u, c * P:(c + 1) * P], query[:, u, :],
                                                 start=True, stop=True)
                        m.then_inc(s_sc, 1)

            def weighted_values(b, q):
                for u in range(4):
                    n = (b * QUADS + q) * 4 + u
                    pe.wait_ge(s_w, n + 1)
                    pe.wait_ge(s_av_free, n + 1)
                    for c in range(NC):
                        lhsT = vt[:, c, 2 * q + u // 2, u % 2:u % 2 + 2, :].rearrange("p i e -> p (i e)")
                        m = nc.tensor.matmul(av[:, u % 2, :], lhsT, w[:, u, c, :], start=(c == 0), stop=(c == NC - 1))
                    m.then_inc(s_av, 1)

            def output(b):
                n = out_base(b)
                bank_free(n)
                pe.wait_ge(s_hT, QUADS * (b + 1))
                for g in range(PAIRS):
                    m = nc.tensor.matmul(pj[:, 0, :], wout[:, g, :], hT[:, g, :], start=(g == 0), stop=(g == PAIRS - 1))
                m.then_inc(s_pj, 1)
                bank_free(n + 1)
                pe.wait_ge(s_pj_free, n + 1)
                for c in range(NC):
                    m = nc.tensor.transpose(pj[:, 1, c * P:(c + 1) * P], oT[:, c * P:(c + 1) * P], ident[:, :])
                m.then_inc(s_pj, 1)

            values(0)
            projections(0, 0)
            distances(0, 0)
            with pe.Fori(0, B - 1) as b:
                for q in range(1, QUADS):
                    projections(b, q)
                    weighted_values(b, q - 1)
                    distances(b, q)
                projections_next = b + 1
                weighted = QUADS - 1
                weighted_values(b, weighted)
                values(projections_next)
                projections(projections_next, 0)
                distances(projections_next, 0)
                output(b)
            for q in range(1, QUADS):
                projections(B - 1, q)
                weighted_values(B - 1, q - 1)
                distances(B - 1, q)
            weighted_values(B - 1, QUADS - 1)
            output(B - 1)

        @block.vector
        def _(dve):
            dve.wait_ge(s_in, 16 * N_IN)

            def norm(b, u):
                if not isinstance(b, int):
                    dve.wait_ge(s_xnT_ps, b - 1)
                layernorm_batch(nc, dve, x, b, xn[:, u], stats[:, u], mv[:, u], std[:, u], rstd[:, u],
                                b, s_stats, s_mv, s_std, s_rstd, s_xn, holder[:, :])

            for u in range(2):
                norm(u, u)
            with dve.Fori(1, B // 2) as h:
                for u in range(2):
                    norm(2 * h + u, u)

            def bank_out(n):
                dve.wait_ge(s_pj, n + 1)

            def values(b):
                n = head_base(b)
                for c in range(NC):
                    for h in range(2):
                        bank_out(n + 2 * c + h)
                        nc.vector.tensor_tensor(vt[:, c, 4 * h:4 * h + 4, 0:3:2, :],
                                                pj[:, h, :].rearrange("p (g v e) -> p g v e", v=2, e=E0),
                                                bv[:, h * T:(h + 1) * T].rearrange("p (g v e) -> p g v e", v=2, e=E0),
                                                ALU.add).then_inc(s_pj_free, 1)

            def projections(b, q):
                n = quad_base(b, q)
                for r in range(2):
                    g = (b * QUADS + q) * 2 + r
                    u = 2 * r
                    for i in range(2):
                        bank_out(n + 3 * r + i)
                        if not isinstance(g, int) or g >= 1:
                            dve.wait_ge(s_sq, 2 * g + i - 1)
                            dve.wait_ge(s_split, 2 * g)
                        nc.vector.tensor_scalar(qk[:, i, :], pj[:, (3 * r + i) % 2, :], bqkg[:, 2 * q + r, i:i + 1],
                                                None, ALU.add).then_inc(s_pj_free, 1)
                    bank_out(n + 3 * r + 2)
                    nc.vector.tensor_scalar(gT[:, 2 * q + r, :], pj[:, (3 * r + 2) % 2, :], bqkg[:, 2 * q + r, 2:3],
                                            None, ALU.add).then_inc(s_pj_free, 1)
                    dve.wait_ge(s_pj_free, n + 3 * r + 2)
                    for v in range(2):
                        nc.vector.tensor_scalar(query[0:64, u + v, :], qk[64 * v:64 * v + 64, 0, :], -2.0, None, ALU.mult)
                        nc.vector.tensor_copy(key[0:64, u + v, :], qk[64 * v:64 * v + 64, 1, :]).then_inc(s_split, 1)
                for r in range(2):
                    u = 2 * r
                    bank_out(n + 6 + r)
                    for v in range(2):
                        nc.vector.tensor_copy(query[64:65, u + v, :], pj[32 * v:32 * v + 1, r, :])
                    nc.vector.tensor_copy(key[96:97, u, :], pj[64:65, r, :])
                    nc.vector.tensor_copy(key[96:97, u + 1, :], pj[96:97, r, :]).then_inc(s_pj_free, 1)

            def distances(b, q, u):
                for h in range(2):
                    n = ((b * QUADS + q) * 4 + u) * 2 + h
                    dve.wait_ge(s_sc, n + 1)
                    nc.vector.tensor_scalar(w[:, u, 2 * h:2 * h + 2, :], sc[:, h, :, :], 0.0, None,
                                            ALU.max).then_inc(s_d2, 1)

            def weighted_values(b, q):
                j = b * QUADS + q
                for u in range(4):
                    n = j * 4 + u
                    lo, row = (0, 64) if u % 2 == 0 else (64, 0)
                    g = 2 * q + u // 2
                    dve.wait_ge(s_av, n + 1)
                    if u == 0 and (not isinstance(j, int) or j >= 1):
                        dve.wait_ge(s_sum_out, 32 * j)
                    nc.vector.tensor_copy(srow[row:row + 1, u // 2, :], av[row:row + 1, u % 2, :]).then_inc(s_srow, 1)
                    dve.wait_ge(s_pj_free, quad_base(b, q) + 3 * (u // 2) + 3)
                    nc.vector.tensor_tensor(gT[lo:lo + 64, g, :], av[lo:lo + 64, u % 2, :], gT[lo:lo + 64, g, :],
                                            ALU.mult).then_inc(s_av_free, 1)

            def reciprocals(b, q):
                j = b * QUADS + q
                dve.wait_ge(s_sum_in, 16 * (j + 1))
                nc.vector.tensor_scalar(ssum[:, :], ssum[:, :], ATT_EPS, None, ALU.add).then_inc(s_sume, 1)
                dve.wait_ge(s_sume, j + 1)
                if not isinstance(j, int) or j >= 1:
                    dve.wait_ge(s_rec_out, 16 * j)
                nc.vector.reciprocal(srec[:, :], ssum[:, :]).then_inc(s_rec, 1)

            def normalize(b, q):
                j = b * QUADS + q
                dve.wait_ge(s_bc, 32 * (j + 1))
                dve.wait_ge(s_av_free, 4 * (j + 1) + 2)
                nc.vector.tensor_tensor(hT[:, 2 * q:2 * q + 2, :], hT[:, 2 * q:2 * q + 2, :],
                                        gT[:, 2 * q:2 * q + 2, :], ALU.mult).then_inc(s_hT, 1)

            def output(b):
                n = out_base(b)
                bank_out(n)
                nc.vector.tensor_scalar(oT[:, :], pj[:, 0, :], bout[:, 0:1], None, ALU.add).then_inc(s_pj_free, 1)
                bank_out(n + 1)
                xc = x[:, bass.ds(b * NC, NC), :]
                nc.vector.tensor_tensor(xc, xc, pj[:, 1, :].rearrange("p (c d) -> p c d", c=NC),
                                        ALU.add).then_inc(s_pj_free, 1)

            def quad(b, q, pb, pq):
                if pq is not None and q == 0:
                    weighted_values(pb, pq)
                    values(b)
                projections(b, q)
                if pq is not None and q:
                    weighted_values(pb, pq)
                distances(b, q, 0)
                if pq is not None:
                    reciprocals(pb, pq)
                for u in range(1, 4):
                    distances(b, q, u)
                if pq is not None:
                    normalize(pb, pq)

            for u in range(2):
                nc.vector.memset(av[:, u, :], 0.0).then_inc(s_av_free, 1)
            dve.wait_ge(s_ones, 5)
            values(0)
            quad(0, 0, None, None)
            with dve.Fori(0, B - 1) as b:
                for q in range(1, QUADS):
                    quad(b, q, b, q - 1)
                quad(b + 1, 0, b, QUADS - 1)
                output(b)
            for q in range(1, QUADS):
                quad(B - 1, q, B - 1, q - 1)
            weighted_values(B - 1, QUADS - 1)
            reciprocals(B - 1, QUADS - 1)
            normalize(B - 1, QUADS - 1)
            output(B - 1)

        @block.scalar
        def _(act):
            with act.Fori(0, B // 2) as h:
                for u in range(2):
                    b = 2 * h + u
                    root(nc, act, std[:, u, :], mv[:, u], b, s_mv, s_std)
                    act.wait_ge(s_xnT_ps, b + 1)
                    nc.scalar.copy(xnT[:, bass.ds(b, 1), :].rearrange("p o t -> p (o t)"), pj[:, u, :]).then_inc(s_xnT, 1)

            def weights(j):
                for u in range(4):
                    act.wait_ge(s_d2, 2 * (j * 4 + u + 1))
                    nc.scalar.activation(w[:, u, :, :], w[:, u, :, :], ACT.Sqrt).then_inc(s_sqrt, 1)

                def ln(u):
                    act.wait_ge(s_sqrt, j * 4 + u + 1)
                    nc.scalar.activation(w[:, u, :, :], w[:, u, :, :], ACT.Ln, bias=ATT_EPS).then_inc(s_ln, 1)

                ln(0)
                for u in range(4):
                    if u < 3:
                        ln(u + 1)
                    act.wait_ge(s_ln, j * 4 + u + 1)
                    nc.scalar.activation(w[:, u, :, :], w[:, u, :, :], ACT.Exp, scale=-2.0).then_inc(s_w, 1)

            with act.Fori(0, B * QUADS) as j:
                weights(j)


def layernorm_batch(nc, dve, x, b, xn, stats, mv, std, rstd, n, s_stats, s_mv, s_std, s_rstd, s_xn, holder):
    nc.vector.memset(holder, 0.0)
    for c in range(NC):
        nc.vector.bn_stats(stats[:, c, :], chunk(x, b, c)).then_inc(s_stats, 1)
    dve.wait_ge(s_stats, NC * (n + 1))
    nc.vector.memset(holder, 0.0)
    for c in range(NC):
        nc.vector.bn_aggr(mv[:, c, :], stats[:, c, :]).then_inc(s_mv, 1)
    dve.wait_ge(s_std, n + 1)
    nc.vector.reciprocal(rstd, std).then_inc(s_rstd, 1)
    dve.wait_ge(s_rstd, n + 1)
    for c in range(NC):
        nc.vector.tensor_scalar(xn[:, c, :], chunk(x, b, c), mv[:, c, 0:1], rstd[:, c:c + 1],
                                ALU.subtract, ALU.mult).then_inc(s_xn, 1)


def root(nc, act, std, mv, n, s_mv, s_std):
    act.wait_ge(s_mv, NC * (n + 1))
    nc.scalar.activation(std, mv[:, :, 1], ACT.Sqrt, bias=LN_EPS).then_inc(s_std, 1)


def chunk(x, b, c):
    return x[:, bass.ds(b * NC + c, 1), :].rearrange("p o d -> p (o d)")


def build_rest(nc, a, x, ident, out):
    with ExitStack() as ctx:
        def sb(name, shape):
            return ctx.enter_context(nc.sbuf_tensor(name, shape, F32))

        def psum(name, shape):
            return ctx.enter_context(nc.psum_tensor(name, shape, F32))

        def sem(name):
            return ctx.enter_context(nc.semaphore(name))

        w1 = sb("w1", [P, NE, FF])
        w2 = sb("w2", [P, NE * NF, D])
        b1 = sb("b1", [P, NE * NF])
        b2 = sb("b2", [NE, D])
        wr = sb("wr", [P, NE])
        br = sb("br", [P, NE])
        wq = sb("wq", [P, D])
        bq = sb("bq", [P, 1])
        wkv = sb("wkv", [P, 2 * D])
        bkv = sb("bkv", [P, 2 * D])
        wo = sb("wo", [P, D])
        bo = sb("bo", [P, D])
        wrt = sb("wrt", [P, D])
        wblk = sb("wblk", [P, D])
        dec = sb("dec", [P, NC])
        hmask = sb("hmask", [P, D + H1])
        etri = sb("etri", [P, NE, NE])
        ttri = sb("ttri", [P, (2 * NC - 1) * P])

        holder = sb("holder2", [P, 1])
        stats = sb("stats2", [P, NC, 6])
        mv = sb("mv2", [P, NC, 2])
        std = sb("std2", [P, NC])
        rstd = sb("rstd2", [P, NC])
        xn = sb("xn2", [P, NC, D])
        xb = sb("xb2", [P, T])
        lg = sb("lg", [P, NC, NE])
        pr = sb("pr", [P, NC, NE])
        m4 = sb("m4", [P, NC])
        i4 = sb("i4", [P, NC])
        gt = sb("gt", [P, NC, NE, NE])
        eq = sb("eq", [P, NC, NE, NE])
        rank = sb("rank", [P, NC, NE])
        rw = sb("rw", [P, NC, NE])
        rwT = sb("rwT", [NE, T])
        hr = sb("hr", [P, 2, T])
        hm = sb("hm", [P, 2, T])
        yT = sb("yT", [P, T])
        qT = sb("qT", [P, T])
        kv = sb("kv", [P, NC, 2 * D + 1])
        kvm = sb("kvm", [P, D + H1])
        den = sb("den", [P, NC, H1])
        rden = sb("rden", [P, NC, H1])
        o1 = sb("o1", [P, NC, D])
        o1T = sb("o1T", [P, T])
        prod = sb("prod", [P, NC, D])
        score = sb("score", [P, NC])
        scr = sb("scr", [P, 2, NC, T])
        above = sb("above", [P, 2, NC])
        keep = sb("keep", [P, 2, NC])
        gel = sb("gel", [P, NC, D])
        res = sb("res", [P, NC, D])

        tp = psum("tp", [P, T])
        z = psum("z", [P, 2, T])
        y = psum("y", [P, T])
        rb = psum("rb", [P, 2, T])
        sm = psum("sm", [P, T])

        names = """in2 ones2 stats2 mv2 std2 rstd2 xn2 xnT2 xb2 logits chain exp rw rwT_ps rwT rb z hr hm y yT yT_ps
                 x2 qT_ps qT kv_ps kv kvm_ps kvm nd_ps o1 o1T_ps o1T y1_ps score_ps score_col blk gel res out_dma""".split()
        S = {n: sem("s_" + n) for n in names}
        loads = [
            (w1[:, :, :], a["W1"].rearrange("e d f -> d e f")),
            (w2[:, :, :], a["W2"].rearrange("e (k p) d -> p (e k) d", p=P)),
            (b1[:, :], a["b1"]), (b2[:, :], a["b2"]), (wr[:, :], a["Wr"]),
            (br[:, :], a["br"].partition_broadcast(P)),
            (wq[:, :], a["W_q"]), (bq[:, :], a["b_q"].rearrange("(p o) -> p o", o=1)),
            (wkv[:, :], a["W_kv"]), (bkv[:, :], a["b_kv"].partition_broadcast(P)),
            (wo[:, :], a["W_o"]), (bo[:, :], a["b_o"].partition_broadcast(P)),
            (wrt[:, :], a["w_router"].partition_broadcast(P)), (wblk[:, :], a["w_block"]),
            (dec[:, :], a["c_dec"]), (hmask[:, :], a["c_hmask"]), (etri[:, :, :], a["c_etri"]),
            (ttri[:, :], a["c_ttri"]),
        ]
        NLN = 3
        N_CHAIN = 26

        def over(t, n):
            t = t[tuple(slice(None) for _ in t.shape)]
            return t.unsqueeze(len(t.shape)).to_broadcast(list(t.shape) + [n])

        def every(t, n):
            t = t[tuple(slice(None) for _ in t.shape)]
            return t.unsqueeze(1).to_broadcast([t.shape[0], n] + list(t.shape[1:]))

        block = ctx.enter_context(nc.Block())

        @block.sync
        def _(sp):
            for dst, src in loads:
                sp.dma_start(dst, src).then_inc(S["in2"], 16)
            with sp.Fori(0, B) as b:
                sp.wait_ge(S["res"], b + 1)
                sp.dma_start(out[bass.ds(b, 1)].rearrange("o (c p) d -> p (o c) d", p=P), res[:, :, :]).then_inc(S["out_dma"], 16)
            sp.wait_ge(S["out_dma"], 16 * B)

        @block.gpsimd
        def _(pool):
            nc.gpsimd.memset(kv[:, :, 2 * D:2 * D + 1], 1.0).then_inc(S["ones2"], 1)

        @block.scalar
        def _(act):
            act.wait_ge(S["in2"], 16 * len(loads))
            with act.Fori(0, B) as b:
                def turned(n):
                    act.wait_ge(S["xnT2"], NLN * b + n + 1)
                    nc.scalar.copy(xb[:, :], tp[:, :]).then_inc(S["xb2"], 1)

                def rooted(n):
                    root(nc, act, std[:, :], mv, NLN * b + n, S["mv2"], S["std2"])

                rooted(0)
                turned(0)
                act.wait_ge(S["chain"], N_CHAIN * b + 3)
                nc.scalar.activation(pr[:, :, :], lg[:, :, :], ACT.Exp).then_inc(S["exp"], 1)
                act.wait_ge(S["rwT_ps"], b + 1)
                nc.scalar.copy(rwT[:, :], tp[0:NE, :]).then_inc(S["rwT"], 1)
                for k in range(NE * NF):
                    n = b * NE * NF + k
                    act.wait_ge(S["z"], n + 1)
                    if k >= 2:
                        act.wait_ge(S["hm"], n - 1)
                    nc.scalar.activation(hr[:, k % 2, :], z[:, k % 2, :], ACT.Relu, bias=b1[:, k:k + 1]).then_inc(S["hr"], 1)
                act.wait_ge(S["y"], b + 1)
                nc.scalar.copy(yT[:, :], y[:, :]).then_inc(S["yT"], 1)
                rooted(1)
                turned(1)
                act.wait_ge(S["qT_ps"], b + 1)
                nc.scalar.activation(qT[:, :], y[:, :], ACT.Relu, bias=bq[:, 0:1]).then_inc(S["qT"], 1)
                act.wait_ge(S["o1T_ps"], b + 1)
                nc.scalar.copy(o1T[:, :], tp[:, :]).then_inc(S["o1T"], 1)
                rooted(2)
                turned(2)
                act.wait_ge(S["blk"], b + 1)
                nc.scalar.activation(gel[:, :, :], y[:, :].rearrange("p (c d) -> p c d", c=NC),
                                     ACT.Gelu_apprx_tanh).then_inc(S["gel"], 1)

        @block.tensor
        def _(pe):
            pe.wait_ge(S["in2"], 16 * len(loads))
            with pe.Fori(0, B) as b:
                def turn(n):
                    pe.wait_ge(S["xn2"], NC * (NLN * b + n + 1))
                    for c in range(NC):
                        m = nc.tensor.transpose(tp[:, c * P:(c + 1) * P], xn[:, c, :], ident[:, :])
                    m.then_inc(S["xnT2"], 1)
                    pe.wait_ge(S["xb2"], NLN * b + n + 1)

                turn(0)
                for c in range(NC):
                    m = nc.tensor.matmul(sm[:, c * NE:(c + 1) * NE], xb[:, c * P:(c + 1) * P], wr[:, :],
                                         start=(c == 0), stop=True, skip_group_check=True)
                m.then_inc(S["logits"], 1)
                pe.wait_ge(S["rw"], b + 1)
                for c in range(NC):
                    m = nc.tensor.transpose(tp[0:NE, c * P:(c + 1) * P], rw[:, c, :], ident[:, :])
                m.then_inc(S["rwT_ps"], 1)

                def spread(e):
                    if e >= 2:
                        pe.wait_ge(S["hm"], b * NE * NF + (e - 1) * NF)
                    for c in range(NC):
                        m = nc.tensor.transpose(rb[:, e % 2, c * P:(c + 1) * P],
                                                rw[:, c, e:e + 1].to_broadcast([P, P]), ident[:, :])
                    m.then_inc(S["rb"], 1)

                def hidden(k):
                    n = b * NE * NF + k
                    if k >= 2:
                        pe.wait_ge(S["hr"], n - 1)
                    nc.tensor.matmul(z[:, k % 2, :], w1[:, k // NF, (k % NF) * P:(k % NF + 1) * P], xb[:, :],
                                     start=True, stop=True).then_inc(S["z"], 1)

                spread(0)
                hidden(0)
                hidden(1)
                pe.wait_ge(S["rwT"], b + 1)
                nc.tensor.matmul(y[:, :], b2[:, :], rwT[:, :], start=True, stop=False)
                for k in range(NE * NF):
                    if k % NF == 0 and k // NF + 1 < NE:
                        spread(k // NF + 1)
                    pe.wait_ge(S["hm"], b * NE * NF + k + 1)
                    m = nc.tensor.matmul(y[:, :], w2[:, k, :], hm[:, k % 2, :], start=False, stop=(k == NE * NF - 1))
                    if k + 2 < NE * NF:
                        hidden(k + 2)
                m.then_inc(S["y"], 1)
                pe.wait_ge(S["yT"], b + 1)
                for c in range(NC):
                    m = nc.tensor.transpose(tp[:, c * P:(c + 1) * P], yT[:, c * P:(c + 1) * P], ident[:, :])
                m.then_inc(S["yT_ps"], 1)

                turn(1)
                nc.tensor.matmul(y[:, :], wq[:, :], xb[:, :], start=True, stop=True).then_inc(S["qT_ps"], 1)
                for c in range(NC):
                    m = nc.tensor.matmul(z[:, c // 2, (c % 2) * 2 * D:(c % 2 + 1) * 2 * D], xb[:, c * P:(c + 1) * P],
                                         wkv[:, :], start=(c % 2 == 0), stop=True, skip_group_check=True)
                m.then_inc(S["kv_ps"], 1)
                pe.wait_ge(S["kv"], b + 1)
                for c in range(NC):
                    m = nc.tensor.matmul(sm[:, 0:D + 1], kv[:, c, 0:D], kv[:, c, D:2 * D + 1], start=(c == 0), stop=(c == NC - 1))
                m.then_inc(S["kvm_ps"], 1)
                pe.wait_ge(S["kvm"], b + 1)
                pe.wait_ge(S["qT"], b + 1)
                for c in range(NC):
                    m = nc.tensor.matmul(z[:, c // 2, (c % 2) * 2 * D:(c % 2) * 2 * D + D + H1], qT[:, c * P:(c + 1) * P],
                                         kvm[:, :], start=(c % 2 == 0), stop=True, skip_group_check=True)
                m.then_inc(S["nd_ps"], 1)
                pe.wait_ge(S["o1"], b + 1)
                for c in range(NC):
                    m = nc.tensor.transpose(tp[:, c * P:(c + 1) * P], o1[:, c, :], ident[:, :])
                m.then_inc(S["o1T_ps"], 1)
                pe.wait_ge(S["o1T"], b + 1)
                for c in range(NC):
                    m = nc.tensor.matmul(y[:, c * P:(c + 1) * P], o1T[:, c * P:(c + 1) * P], wo[:, :],
                                         start=(c == 0), stop=True, skip_group_check=True)
                m.then_inc(S["y1_ps"], 1)

                turn(2)
                for c in range(NC):
                    m = nc.tensor.matmul(y[:, c * P:(c + 1) * P], xb[:, c * P:(c + 1) * P], wblk[:, :],
                                         start=(c == 0), stop=True, skip_group_check=True)
                m.then_inc(S["blk"], 1)
                pe.wait_ge(S["score_col"], b + 1)
                for c in range(NC):
                    m = nc.tensor.transpose(sm[:, c * P:(c + 1) * P], score[:, c:c + 1].to_broadcast([P, P]), ident[:, :])
                m.then_inc(S["score_ps"], 1)

        @block.vector
        def _(dve):
            dve.wait_ge(S["in2"], 16 * len(loads))
            dve.wait_ge(S["ones2"], 1)
            V = nc.vector
            with dve.Fori(0, B) as b:
                done = [0]

                def link(ins):
                    done[0] += 1
                    ins.then_inc(S["chain"], 1)
                    dve.wait_ge(S["chain"], N_CHAIN * b + done[0])

                def norm(n):
                    layernorm_batch(nc, dve, x, b, xn[:, :, :], stats, mv, std[:, :], rstd[:, :], NLN * b + n,
                                    S["stats2"], S["mv2"], S["std2"], S["rstd2"], S["xn2"],
                                    holder[:, :])

                norm(0)
                dve.wait_ge(S["logits"], b + 1)
                link(V.tensor_tensor(lg[:, :, :], sm[:, 0:NC * NE].rearrange("p (c e) -> p c e", c=NC),
                                     every(br, NC), ALU.add))
                link(V.tensor_reduce(m4[:, :], lg[:, :, :], AX.X, ALU.max))
                link(V.tensor_tensor(lg[:, :, :], lg[:, :, :], over(m4, NE), ALU.subtract))
                dve.wait_ge(S["exp"], b + 1)
                link(V.tensor_reduce(m4[:, :], pr[:, :, :], AX.X, ALU.add))
                link(V.reciprocal(i4[:, :], m4[:, :]))
                link(V.tensor_tensor(pr[:, :, :], pr[:, :, :], over(i4, NE), ALU.mult))
                pj_ = pr[:, :, :].unsqueeze(2).to_broadcast([P, NC, NE, NE])
                pe_ = over(pr, NE)
                V.tensor_tensor(gt[:, :, :, :], pj_, pe_, ALU.is_gt)
                link(V.tensor_tensor(eq[:, :, :, :], pj_, pe_, ALU.is_equal))
                link(V.tensor_tensor(eq[:, :, :, :], eq[:, :, :, :], every(etri, NC), ALU.mult))
                link(V.tensor_tensor(gt[:, :, :, :], gt[:, :, :, :], eq[:, :, :, :], ALU.add))
                link(V.tensor_reduce(rank[:, :, :], gt[:, :, :, :], AX.X, ALU.add))
                link(V.scalar_tensor_tensor(rw[:, :, :], rank[:, :, :], float(TOP_K), pr[:, :, :], ALU.is_lt, ALU.mult))
                link(V.tensor_reduce(m4[:, :], rw[:, :, :], AX.X, ALU.add))
                link(V.reciprocal(i4[:, :], m4[:, :]))
                V.tensor_tensor(rw[:, :, :], rw[:, :, :], over(i4, NE), ALU.mult).then_inc(S["rw"], 1)
                for k in range(NE * NF):
                    n = b * NE * NF + k
                    if k % NF == 0:
                        dve.wait_ge(S["rb"], b * NE + k // NF + 1)
                    dve.wait_ge(S["hr"], n + 1)
                    V.tensor_tensor(hm[:, k % 2, :], hr[:, k % 2, :], rb[:, (k // NF) % 2, :], ALU.mult).then_inc(S["hm"], 1)
                dve.wait_ge(S["yT_ps"], b + 1)
                xc = x[:, bass.ds(b * NC, NC), :]
                nat = "p (c d) -> p c d"
                link(V.tensor_tensor(xc, xc, tp[:, :].rearrange(nat, c=NC), ALU.add))

                norm(1)
                dve.wait_ge(S["kv_ps"], b + 1)
                link(V.tensor_tensor(kv[:, :, 0:2 * D], z[:, :, :].rearrange("p g (c d) -> p (g c) d", c=2),
                                     every(bkv, NC), ALU.add))
                V.scalar_tensor_tensor(kv[:, :, 0:D], kv[:, :, 0:D], 0.0, over(dec, D), ALU.max, ALU.mult).then_inc(S["kv"], 1)
                dve.wait_ge(S["kvm_ps"], b + 1)
                V.tensor_tensor(kvm[:, 0:D], sm[:, 0:D], hmask[:, 0:D], ALU.mult)
                V.tensor_scalar(kvm[:, D:D + H1], hmask[:, D:D + H1], sm[:, D:D + 1], None, ALU.mult).then_inc(S["kvm"], 1)
                dve.wait_ge(S["nd_ps"], b + 1)
                nd = z[:, :, :].rearrange("p g (c d) -> p (g c) d", c=2)
                link(V.tensor_tensor(den[:, :, :], nd[:, :, D:D + H1], over(dec, H1), ALU.mult))
                link(V.tensor_scalar(den[:, :, :], den[:, :, :], LIN_EPS, None, ALU.add))
                link(V.reciprocal(rden[:, :, :], den[:, :, :]))
                link(V.tensor_tensor(rden[:, :, :], rden[:, :, :], over(dec, H1), ALU.mult))
                V.tensor_tensor(o1[:, :, :].rearrange("p c (h e) -> p c h e", e=E1),
                                nd[:, :, 0:D].rearrange("p c (h e) -> p c h e", e=E1), over(rden, E1), ALU.mult).then_inc(S["o1"], 1)
                dve.wait_ge(S["y1_ps"], b + 1)
                link(V.tensor_tensor(prod[:, :, :], y[:, :].rearrange(nat, c=NC), every(bo, NC), ALU.add))
                link(V.tensor_tensor(xc, xc, prod[:, :, :], ALU.add))

                norm(2)
                dve.wait_ge(S["xn2"], NC * NLN * (b + 1))
                link(V.tensor_tensor(prod[:, :, :], xn[:, :, :], every(wrt, NC), ALU.mult))
                V.tensor_reduce(score[:, :], prod[:, :, :], AX.X, ALU.add).then_inc(S["score_col"], 1)
                dve.wait_ge(S["score_ps"], b + 1)
                for c in range(NC):
                    V.tensor_scalar(scr[:, 0, c, :], sm[:, :], score[:, c:c + 1], None, ALU.is_gt, ALU.add, accum_out=above[:, 0, c:c + 1])
                    ins = V.scalar_tensor_tensor(scr[:, 1, c, :], sm[:, :], score[:, c:c + 1],
                                                 ttri[:, (NC - 1 - c) * P:(2 * NC - 1 - c) * P], ALU.is_equal, ALU.mult,
                                                 accum_out=above[:, 1, c:c + 1])
                link(ins)
                link(V.tensor_tensor(above[:, 0, :], above[:, 0, :], above[:, 1, :], ALU.add))
                V.tensor_scalar(keep[:, 0, :], above[:, 0, :], float(KEEP), None, ALU.is_lt)
                link(V.tensor_scalar(keep[:, 1, :], above[:, 0, :], float(KEEP), None, ALU.is_ge))
                dve.wait_ge(S["gel"], b + 1)
                dve.wait_ge(S["out_dma"], 16 * b)
                for c in range(NC):
                    ins = V.scalar_tensor_tensor(res[:, c, :], xn[:, c, :], keep[:, 1, c:c + 1], chunk(x, b, c), ALU.mult, ALU.add)
                link(ins)
                for c in range(NC):
                    ins = V.scalar_tensor_tensor(res[:, c, :], gel[:, c, :], keep[:, 0, c:c + 1], res[:, c, :], ALU.mult, ALU.add)
                ins.then_inc(S["res"], 1)
                assert done[0] == N_CHAIN, done[0]


def constants():
    f = np.float32
    nsel = np.zeros((P, 2, P), f)
    for i in range(2):
        for v in range(2):
            nsel[64 * v:64 * v + 64, i, 64 * i + 32 * v] = 1
    head = np.arange(D) // E1
    hmask = np.concatenate([head[:, None] == head[None, :], head[:, None] == np.arange(H1)[None, :]], 1).astype(f)
    e = np.arange(NE)
    etri = np.broadcast_to((e[None, :] < e[:, None]).astype(f), (P, NE, NE)).copy()
    j = np.arange((2 * NC - 1) * P) - (NC - 1) * P
    ttri = (j[None, :] < np.arange(P)[:, None]).astype(f)
    dec = np.exp(-np.arange(T, dtype=f) / f(T)).astype(f).reshape(NC, P).T.copy()
    return {"c_ident": np.eye(P, dtype=f), "c_nsel": nsel, "c_hmask": hmask, "c_etri": etri, "c_ttri": ttri, "c_dec": dec}


def kernel(**inputs):
    import concourse.bacc as _bacc
    from concourse.bass_utils import run_bass_kernel_spmd as _run

    i = {k: np.ascontiguousarray(v) for k, v in inputs.items()}
    win = i["L0_attn_W_in"].reshape(D, PAIRS, 2, 4, E0)
    bin_ = i["L0_attn_b_in"].reshape(PAIRS, 2, 4, E0)
    arrays = {
        "X": i["L0_attn_X"].reshape(B * T, D),
        "W_qkg": win[:, :, :, [0, 1, 3]].transpose(0, 1, 3, 2, 4).reshape(D, PAIRS, 3, P),
        "b_qkg": bin_[:, :, [0, 1, 3]].transpose(1, 3, 0, 2).reshape(P, PAIRS, 3),
        "W_v": win[:, :, :, 2].reshape(D, H0 * E0),
        "b_v": bin_[:, :, 2].reshape(H0 * E0),
        "W_out": i["L0_attn_W_out"], "b_out": i["L0_attn_b_out"],
        "W1": i["L0_ffn_W1"], "b1": i["L0_ffn_b1"].reshape(NE * NF, P).T,
        "W2": i["L0_ffn_W2"], "b2": i["L0_ffn_b2"], "Wr": i["L0_ffn_Wr"], "br": i["L0_ffn_br"],
        "W_q": i["L1_attn_W_q"].T, "b_q": i["L1_attn_b_q"],
        "W_kv": np.concatenate([i["L1_attn_W_k"].T, i["L1_attn_W_v"].T], 1),
        "b_kv": np.concatenate([i["L1_attn_b_k"], i["L1_attn_b_v"]]),
        "W_o": i["L1_attn_W_o"].T, "b_o": i["L1_attn_b_o"],
        "w_router": i["L1_ffn_w_router"], "w_block": i["L1_ffn_w_block"],
        **constants(),
    }
    arrays = {k: np.ascontiguousarray(v) for k, v in arrays.items()}
    nc = _bacc.Bacc("TRN2", target_bir_lowering=False, num_devices=1)
    a = {k: nc.dram_tensor(f"in_{k}", v.shape, F32, kind="ExternalInput").ap() for k, v in arrays.items()}
    out = nc.dram_tensor("out", (B, T, D), F32, kind="ExternalOutput").ap()
    build(nc, a, out)
    r = _run(nc, [{f"in_{k}": v for k, v in arrays.items()}], core_ids=[0])
    return r.results[0]["out"]
```

```python
from contextlib import ExitStack

import numpy as np

import concourse.bass as bass
from concourse import mybir

ALU = mybir.AluOpType
ACT = mybir.ActivationFunctionType
AX = mybir.AxisListType
F32 = mybir.dt.float32
F32R = mybir.dt.float32r

P = 128
B, T, D = 8, 512, 128
NC = T // P
H0, E0 = 16, 64
PAIRS = H0 // 2
QUADS = H0 // 4
ATT_EPS = 1e-4
LN_EPS = 1e-5
NE, FF = 8, 512
NF = FF // P
TOP_K = 2
H1, E1 = 16, 8
LIN_EPS = 1e-6
KEEP = T * 3 // 4

N_QKG, N_SUM, N_V, N_OUT, N_TURN = 6, 2, 2 * NC, 2, 2
N_BATCH = QUADS * (N_QKG + N_SUM) + N_V + N_OUT + N_TURN


def build(nc, a, out):
    def scratch(name, shape):
        return nc.dram_tensor(name, shape, F32, kind="Internal").ap()

    x1 = scratch("x1", (B, P, NC, D))
    dsum = scratch("head_sums", (QUADS, 2, 2, T))
    drec = scratch("head_recips", (QUADS, 2, 2, T))
    build_attention(nc, a, x1, dsum, drec)
    build_rest(nc, a, x1, out)


def product(nc, out, lhsT, rhs, start=True, stop=True):
    for i, (u, v) in enumerate(((0, 0), (1, 0), (0, 1))):
        m = nc.tensor.matmul(out, lhsT[u], rhs[v], start=start and i == 0, stop=stop and i == 2)
    return m


def build_attention(nc, a, x1, dsum, drec):
    with ExitStack() as ctx:
        def sb(name, shape, dt=F32):
            return ctx.enter_context(nc.sbuf_tensor(name, shape, dt))

        def psum(name, shape):
            return ctx.enter_context(nc.psum_tensor(name, shape, F32))

        def sem(name):
            return ctx.enter_context(nc.semaphore(name))

        xa = sb("xa", [P, NC, D])
        stats = sb("stats", [P, NC, 6])
        mv = sb("mv", [P, NC, 2])
        std = sb("std", [P, NC])
        rstd = sb("rstd", [P, NC])
        holder = sb("holder", [P, 1])
        xn = sb("xn", [P, NC, D])
        xs = [sb("xh", [P, T], F32R), sb("xl", [P, T], F32R)]
        wqkg = [sb("wqkg_h", [P, PAIRS, 3, P], F32R), sb("wqkg_l", [P, PAIRS, 3, P], F32R)]
        wv = [sb("wv_h", [P, H0 * E0], F32R), sb("wv_l", [P, H0 * E0], F32R)]
        wout = sb("wout", [P, PAIRS, D])
        bqkg = sb("bqkg", [P, PAIRS, 3])
        bv = sb("bv", [P, H0 * E0])
        bout = sb("bout", [P, 1])
        ident = sb("ident1", [P, P])
        nsel = sb("nsel", [P, 2, P])
        qk = sb("qk", [P, 2, T])
        sq = sb("sq", [P, 2, 2, T])
        query = sb("query", [P, 4, T])
        key = sb("key", [P, 4, T])
        gT = sb("gT", [P, PAIRS, T])
        hT = sb("hT", [P, PAIRS, T])
        vt = sb("vt", [P, NC, PAIRS, 3, E0])
        w = sb("w", [P, 2, 4, NC, T])
        srow = sb("srow", [P, 2, T])
        ssum = sb("ssum", [P, 2 * 2 * T // P])
        srec = sb("srec", [P, 2 * 2 * T // P])
        oT = sb("oT", [P, T])
        xc = sb("xc", [P, NC, D])

        pj = psum("pj", [P, 2, T])
        sc = psum("sc", [P, 2, 2, T])
        av = psum("av", [P, 2, T])

        s_w_in = sem("s_w_in")
        s_in = sem("s_in")
        s_ident = sem("s_ident")
        s_wsplit = sem("s_wsplit")
        s_ones = sem("s_ones")
        s_xa = sem("s_xa")
        s_stats = sem("s_stats")
        s_mv = sem("s_mv")
        s_std = sem("s_std")
        s_rstd = sem("s_rstd")
        s_xn = sem("s_xn")
        s_xs = sem("s_xs")
        s_pj = sem("s_pj")
        s_pj_free = sem("s_pj_free")
        s_split = sem("s_split")
        s_sq = sem("s_sq")
        s_sc = sem("s_sc")
        s_d2 = sem("s_d2")
        s_sqrt = sem("s_sqrt")
        s_ln = sem("s_ln")
        s_w = sem("s_w")
        s_av = sem("s_av")
        s_av_free = sem("s_av_free")
        s_srow = sem("s_srow")
        s_sum_out = sem("s_sum_out")
        s_sum_in = sem("s_sum_in")
        s_sume = sem("s_sume")
        s_rec = sem("s_rec")
        s_rec_out = sem("s_rec_out")
        s_bc = sem("s_bc")
        s_hT = sem("s_hT")
        s_xc = sem("s_xc")
        s_x1_out = sem("s_x1_out")

        N_IN = 5

        def qkg_base(b, q):
            n = (0, N_QKG + N_SUM, 2 * (N_QKG + N_SUM) + N_V, 3 * (N_QKG + N_SUM) + N_V + N_OUT)[q]
            if isinstance(b, int) and b == 0 and q < 3:
                n += N_TURN
            return b * N_BATCH + n

        def norm_base(b, q):
            between = 0
            if q == 2 and not (isinstance(b, int) and b == 0):
                between = N_OUT
            if q == 3 and not (isinstance(b, int) and b == B - 1):
                between = N_TURN
            return qkg_base(b, q) + N_QKG + between

        def v_base(b):
            return norm_base(b, 1) + N_SUM

        def out_base(b):
            if isinstance(b, int) and b == B - 1:
                return norm_base(b, 3) + N_SUM
            return qkg_base(b + 1, 2) + N_QKG

        def turn_base(b):
            if isinstance(b, int) and b == 0:
                return 0
            return qkg_base(b - 1, 3) + N_QKG

        def later(b, q, n):
            return b + (q + n) // QUADS, (q + n) % QUADS

        block = ctx.enter_context(nc.Block())

        @block.sync
        def _(sp):
            X = a["X"].rearrange("(b c p) d -> b p c d", c=NC, p=P)

            def load_x(tile, b, sem):
                sp.dma_start(tile[:, :, :], X[bass.ds(b, 1)].rearrange("o p c d -> p (o c) d")).then_inc(sem, 16)

            load_x(xa, 0, s_xa)
            sp.dma_start(ident[:, :], a["c_ident"]).then_inc(s_ident, 16)
            n = PAIRS * 3 * P
            staged = w[:, 1].rearrange("p u c t -> p (u c t)")
            sp.dma_start(staged[:, 0:n], a["W_qkg"].rearrange("p g i e -> p (g i e)")).then_inc(s_w_in, 16)
            sp.dma_start(staged[:, n:n + H0 * E0], a["W_v"]).then_inc(s_w_in, 16)
            sp.dma_start(bqkg[:, :, :], a["b_qkg"]).then_inc(s_in, 16)
            sp.dma_start(nsel[:, :, :], a["c_nsel"]).then_inc(s_in, 16)
            sp.dma_start(bv[:, :], a["b_v"].partition_broadcast(P)).then_inc(s_in, 16)
            sp.dma_start(wout[:, :, :], a["W_out"].rearrange("(g p) d -> p g d", p=P)).then_inc(s_in, 16)
            sp.dma_start(bout[:, :], a["b_out"].rearrange("(p o) -> p o", o=1)).then_inc(s_in, 16)
            load_x(xc, 0, s_xc)

            def normalizer(b, q):
                j = b * QUADS + q
                sp.wait_ge(s_srow, 4 * (j + 1))
                sp.dma_start(dsum[q:q + 1, :, 0, :], srow[64:65, :, :]).then_inc(s_sum_out, 16)
                sp.dma_start(dsum[q:q + 1, :, 1, :], srow[0:1, :, :]).then_inc(s_sum_out, 16)
                sp.wait_ge(s_sum_out, 32 * (j + 1))
                sp.dma_start(ssum[:, :], dsum[q].rearrange("g v t -> (g v t)").rearrange("(p k) -> p k", p=P)).then_inc(s_sum_in, 16)
                sp.wait_ge(s_rec, j + 1)
                sp.dma_start(drec[q].rearrange("g v t -> (g v t)").rearrange("(p k) -> p k", p=P), srec[:, :]).then_inc(s_rec_out, 16)
                sp.wait_ge(s_rec_out, 16 * (j + 1))
                for v in range(2):
                    sp.dma_start(hT[64 * v:64 * v + 64, 2 * q:2 * q + 2, :],
                                 drec[q, :, v, :].partition_broadcast(64)).then_inc(s_bc, 16)

            def store_x1(b):
                sp.wait_ge(s_pj_free, out_base(b) + 2)
                sp.dma_start(x1[bass.ds(b, 1)].rearrange("o p c d -> p (o c) d"), xc[:, :, :]).then_inc(s_x1_out, 16)
                sp.wait_ge(s_x1_out, 16 * (b + 1))

            with sp.Fori(0, B - 1) as b:
                sp.wait_ge(s_xn, NC * (b + 1))
                load_x(xa, b + 1, s_xa)
                for q in range(QUADS):
                    normalizer(b, q)
                store_x1(b)
                load_x(xc, b + 1, s_xc)
            for q in range(QUADS):
                normalizer(B - 1, q)
            store_x1(B - 1)

        @block.gpsimd
        def _(pool):
            nc.gpsimd.memset(query[:, :, :], 0.0).then_inc(s_ones, 1)
            nc.gpsimd.memset(key[:, :, :], 0.0).then_inc(s_ones, 1)
            nc.gpsimd.memset(vt[:, :, :, 1, :], 1.0).then_inc(s_ones, 1)
            pool.wait_ge(s_ones, 3)
            nc.gpsimd.memset(query[96:97, :, :], 1.0).then_inc(s_ones, 1)
            pool.wait_ge(s_ones, 4)
            nc.gpsimd.memset(key[64:65, :, :], 1.0).then_inc(s_ones, 1)
            pool.wait_ge(s_ones, 5)

            def squares(b, q):
                for r in range(2):
                    for i in range(2):
                        pool.wait_ge(s_pj_free, qkg_base(b, q) + 3 * r + i + 1)
                        nc.gpsimd.tensor_tensor(sq[:, r, i, :], qk[:, i, :], qk[:, i, :], ALU.mult).then_inc(s_sq, 1)

            squares(0, 0)
            squares(0, 1)
            squares(0, 2)
            with pool.Fori(0, B - 1) as b:
                squares(b, 3)
                for q in range(3):
                    squares(b + 1, q)
            squares(B - 1, 3)

        @block.tensor
        def _(pe):
            def bank_free(n):
                if not isinstance(n, int) or n >= 2:
                    pe.wait_ge(s_pj_free, n - 1)

            def turn(b):
                n = turn_base(b)
                pe.wait_ge(s_xn, NC * (b + 1))
                for h in range(2):
                    bank_free(n + h)
                    for c in range(2 * h, 2 * h + 2):
                        m = nc.tensor.transpose(pj[:, h, c % 2 * P:(c % 2 + 1) * P], xn[:, c, :], ident[:, :])
                    m.then_inc(s_pj, 1)

            def values(b):
                n = v_base(b)
                for c in range(NC):
                    for h in range(2):
                        bank_free(n + 2 * c + h)
                        product(nc, pj[:, h, :], [x[:, c * P:(c + 1) * P] for x in xs],
                                [v[:, h * T:(h + 1) * T] for v in wv]).then_inc(s_pj, 1)

            def projections(b, q, r):
                n = qkg_base(b, q)
                if q == 0:
                    pe.wait_ge(s_pj_free, turn_base(b) + 2)
                for i in range(3):
                    bank_free(n + 3 * r + i)
                    product(nc, pj[:, (3 * r + i) % 2, :], [m[:, 2 * q + r, i, :] for m in wqkg],
                            [x[:, :] for x in xs]).then_inc(s_pj, 1)

            def sums_of_squares(b, q):
                n = norm_base(b, q)
                for r in range(2):
                    g = (b * QUADS + q) * 2 + r
                    bank_free(n + r)
                    pe.wait_ge(s_sq, 2 * g + 2)
                    nc.tensor.matmul(pj[:, r, :], nsel[:, 0, :], sq[:, r, 0, :], start=True, stop=False)
                    nc.tensor.matmul(pj[:, r, :], nsel[:, 1, :], sq[:, r, 1, :],
                                     start=False, stop=True).then_inc(s_pj, 1)

            def distances(b, q):
                for u in range(4):
                    n = (b * QUADS + q) * 4 + u
                    pe.wait_ge(s_pj_free, norm_base(b, q) + 1 + u // 2)
                    for h in range(2):
                        if not isinstance(n, int) or n >= 1:
                            pe.wait_ge(s_d2, 2 * n + h - 1)
                        for k in range(2):
                            c = 2 * h + k
                            m = nc.tensor.matmul(sc[:, h, k, :], key[:, u, c * P:(c + 1) * P], query[:, u, :],
                                                 start=True, stop=True)
                        m.then_inc(s_sc, 1)

            def weighted_values(b, q, u):
                n = (b * QUADS + q) * 4 + u
                pe.wait_ge(s_w, n + 1)
                pe.wait_ge(s_av_free, n + 1)
                for c in range(NC):
                    lhsT = vt[:, c, 2 * q + u // 2, u % 2:u % 2 + 2, :].rearrange("p i e -> p (i e)")
                    m = nc.tensor.matmul(av[:, u % 2, :], lhsT, w[:, q % 2, u, c, :], start=(c == 0), stop=(c == NC - 1))
                m.then_inc(s_av, 1)

            def output(b):
                n = out_base(b)
                bank_free(n)
                pe.wait_ge(s_hT, QUADS * (b + 1))
                for g in range(PAIRS):
                    m = nc.tensor.matmul(pj[:, 0, :], wout[:, g, :], hT[:, g, :], start=(g == 0), stop=(g == PAIRS - 1))
                m.then_inc(s_pj, 1)

            def turn_output(b):
                n = out_base(b)
                bank_free(n + 1)
                pe.wait_ge(s_pj_free, n + 1)
                for c in range(NC):
                    m = nc.tensor.transpose(pj[:, 1, c * P:(c + 1) * P], oT[:, c * P:(c + 1) * P], ident[:, :])
                m.then_inc(s_pj, 1)

            def body(b, q, first=False, last=False):
                next_quad, last_quad = later(b, q, 1), later(b, q, -1)
                ends = q == 1 and not (isinstance(b, int) and b == 0)
                distances(b, q)
                if not last:
                    projections(*next_quad, 0)
                if not first:
                    weighted_values(*last_quad, 0)
                    weighted_values(*last_quad, 1)
                if not last:
                    projections(*next_quad, 1)
                if ends:
                    output(b - 1)
                if not first:
                    weighted_values(*last_quad, 2)
                if ends:
                    turn_output(b - 1)
                if q == 2 and not (isinstance(b, int) and b == B - 1):
                    turn(b + 1)
                if not last:
                    sums_of_squares(*next_quad)
                if not first:
                    weighted_values(*last_quad, 3)
                if q == 0:
                    values(b)

            pe.wait_ge(s_ident, 16)
            turn(0)
            pe.wait_ge(s_wsplit, 4)
            projections(0, 0, 0)
            projections(0, 0, 1)
            pe.wait_ge(s_in, 16 * N_IN)
            sums_of_squares(0, 0)
            body(0, 0, first=True)
            body(0, 1)
            with pe.Fori(0, B - 1) as b:
                body(b, 2)
                body(b, 3)
                body(b + 1, 0)
                body(b + 1, 1)
            body(B - 1, 2)
            body(B - 1, 3, last=True)
            for u in range(4):
                weighted_values(B - 1, 3, u)
            output(B - 1)
            turn_output(B - 1)

        @block.vector
        def _(dve):
            def bank_out(n):
                dve.wait_ge(s_pj, n + 1)

            def norm_stats(b):
                dve.wait_ge(s_xa, 16 * (b + 1))
                layernorm_stats(nc, dve, xa, 0, stats, mv, b, s_stats, s_mv, holder[:, :])

            def norm_apply(b):
                layernorm_apply(nc, dve, xa, 0, xn, mv, std[:, :], rstd[:, :], b, s_std, s_rstd, s_xn)

            def turned(b):
                n = turn_base(b)
                for h in range(2):
                    bank_out(n + h)
                    half = slice(h * T // 2, (h + 1) * T // 2)
                    nc.vector.tensor_copy(xs[0][:, half], pj[:, h, 0:T // 2]).then_inc(s_xs, 1)
                    dve.wait_ge(s_xs, 2 * b + h + 1)
                    nc.vector.tensor_tensor(xs[1][:, half], pj[:, h, 0:T // 2], xs[0][:, half].bitcast(F32),
                                            ALU.subtract).then_inc(s_pj_free, 1)

            def values(b):
                n = v_base(b)
                for c in range(NC):
                    for h in range(2):
                        bank_out(n + 2 * c + h)
                        heads = "p (g v e) -> p g v e"
                        nc.vector.tensor_tensor(vt[:, c, 4 * h:4 * h + 4, 0:3:2, :],
                                                pj[:, h, :].rearrange(heads, v=2, e=E0),
                                                bv[:, h * T:(h + 1) * T].rearrange(heads, v=2, e=E0),
                                                ALU.add).then_inc(s_pj_free, 1)

            def projections(b, q, r):
                n = qkg_base(b, q)
                j = b * QUADS + q
                g = j * 2 + r
                u = 2 * r
                for i in range(2):
                    bank_out(n + 3 * r + i)
                    if not isinstance(g, int) or g >= 1:
                        dve.wait_ge(s_sq, 2 * g + i - 1)
                        dve.wait_ge(s_split, 2 * g)
                    nc.vector.tensor_scalar(qk[:, i, :], pj[:, (3 * r + i) % 2, :], bqkg[:, 2 * q + r, i:i + 1],
                                            None, ALU.add).then_inc(s_pj_free, 1)
                bank_out(n + 3 * r + 2)
                if q < 3 and (not isinstance(j, int) or j >= QUADS):
                    dve.wait_ge(s_hT, j - 3)
                nc.vector.tensor_scalar(gT[:, 2 * q + r, :], pj[:, (3 * r + 2) % 2, :], bqkg[:, 2 * q + r, 2:3],
                                        None, ALU.add).then_inc(s_pj_free, 1)
                dve.wait_ge(s_pj_free, n + 3 * r + 2)
                for v in range(2):
                    nc.vector.tensor_scalar(query[0:64, u + v, :], qk[64 * v:64 * v + 64, 0, :], -2.0, None, ALU.mult)
                    nc.vector.tensor_copy(key[0:64, u + v, :], qk[64 * v:64 * v + 64, 1, :]).then_inc(s_split, 1)

            def sums_of_squares(b, q):
                n = norm_base(b, q)
                for r in range(2):
                    u = 2 * r
                    bank_out(n + r)
                    for v in range(2):
                        nc.vector.tensor_copy(query[64:65, u + v, :], pj[32 * v:32 * v + 1, r, :])
                    nc.vector.tensor_copy(key[96:97, u, :], pj[64:65, r, :])
                    nc.vector.tensor_copy(key[96:97, u + 1, :], pj[96:97, r, :]).then_inc(s_pj_free, 1)

            def distances(b, q, u):
                for h in range(2):
                    n = ((b * QUADS + q) * 4 + u) * 2 + h
                    dve.wait_ge(s_sc, n + 1)
                    nc.vector.tensor_scalar(w[:, q % 2, u, 2 * h:2 * h + 2, :], sc[:, h, :, :], 0.0, None,
                                            ALU.max).then_inc(s_d2, 1)

            def weighted_values(b, q, u):
                j = b * QUADS + q
                n = j * 4 + u
                lo, row = (0, 64) if u % 2 == 0 else (64, 0)
                g = 2 * q + u // 2
                dve.wait_ge(s_av, n + 1)
                if u == 0 and (not isinstance(j, int) or j >= 1):
                    dve.wait_ge(s_sum_out, 32 * j)
                nc.vector.tensor_copy(srow[row:row + 1, u // 2, :], av[row:row + 1, u % 2, :]).then_inc(s_srow, 1)
                dve.wait_ge(s_pj_free, qkg_base(b, q) + 3 * (u // 2) + 3)
                nc.vector.tensor_tensor(gT[lo:lo + 64, g, :], av[lo:lo + 64, u % 2, :], gT[lo:lo + 64, g, :],
                                        ALU.mult).then_inc(s_av_free, 1)

            def reciprocals(b, q):
                j = b * QUADS + q
                dve.wait_ge(s_sum_in, 16 * (j + 1))
                nc.vector.tensor_scalar(ssum[:, :], ssum[:, :], ATT_EPS, None, ALU.add).then_inc(s_sume, 1)
                dve.wait_ge(s_sume, j + 1)
                nc.vector.reciprocal(srec[:, :], ssum[:, :]).then_inc(s_rec, 1)

            def normalize(b, q):
                j = b * QUADS + q
                dve.wait_ge(s_bc, 32 * (j + 1))
                dve.wait_ge(s_av_free, 4 * (j + 1) + 2)
                nc.vector.tensor_tensor(hT[:, 2 * q:2 * q + 2, :], hT[:, 2 * q:2 * q + 2, :],
                                        gT[:, 2 * q:2 * q + 2, :], ALU.mult).then_inc(s_hT, 1)

            def output(b):
                n = out_base(b)
                bank_out(n)
                nc.vector.tensor_scalar(oT[:, :], pj[:, 0, :], bout[:, 0:1], None, ALU.add).then_inc(s_pj_free, 1)

            def add_output(b):
                n = out_base(b)
                bank_out(n + 1)
                dve.wait_ge(s_xc, 16 * (b + 1))
                nc.vector.tensor_tensor(xc[:, :, :], xc[:, :, :], pj[:, 1, :].rearrange("p (c d) -> p c d", c=NC),
                                        ALU.add).then_inc(s_pj_free, 1)

            def body(b, q, done=2, last=False):
                normed = q == 2 and not (isinstance(b, int) and b == B - 1)
                for u in range(3):
                    distances(b, q, u)
                if done >= 2:
                    reciprocals(*later(b, q, -2))
                if normed:
                    norm_stats(b + 1)
                distances(b, q, 3)
                next_quad, last_quad = later(b, q, 1), later(b, q, -1)
                ends = q == 1 and not (isinstance(b, int) and b == 0)
                if not last:
                    projections(*next_quad, 0)
                if done >= 1:
                    weighted_values(*last_quad, 0)
                if done >= 2:
                    normalize(*later(b, q, -2))
                if done >= 1:
                    weighted_values(*last_quad, 1)
                if normed:
                    norm_apply(b + 1)
                if not last:
                    projections(*next_quad, 1)
                if ends:
                    output(b - 1)
                if done >= 1:
                    weighted_values(*last_quad, 2)
                if ends:
                    add_output(b - 1)
                if normed:
                    turned(b + 1)
                if not last:
                    sums_of_squares(*next_quad)
                if done >= 1:
                    weighted_values(*last_quad, 3)
                if q == 0:
                    values(b)

            norm_stats(0)
            norm_apply(0)
            dve.wait_ge(s_w_in, 32)
            n = 0
            for k, (hi, lo) in enumerate((wqkg, wv)):
                size = (PAIRS * 3 * P, H0 * E0)[k]
                staged = w[:, 1].rearrange("p u c t -> p (u c t)")[:, n:n + size]
                flat = "p g i e -> p (g i e)"
                hi_, lo_ = (hi[:, :, :, :].rearrange(flat), lo[:, :, :, :].rearrange(flat)) if k == 0 else (hi[:, :], lo[:, :])
                nc.vector.tensor_copy(hi_, staged).then_inc(s_wsplit, 1)
                dve.wait_ge(s_wsplit, 2 * k + 1)
                nc.vector.tensor_tensor(lo_, staged, hi_.bitcast(F32), ALU.subtract).then_inc(s_wsplit, 1)
                n += size
            dve.wait_ge(s_wsplit, 4)
            for u in range(2):
                nc.vector.memset(av[:, u, :], 0.0).then_inc(s_av_free, 1)
            dve.wait_ge(s_in, 16 * N_IN)
            dve.wait_ge(s_ones, 5)
            turned(0)
            projections(0, 0, 0)
            projections(0, 0, 1)
            sums_of_squares(0, 0)
            body(0, 0, done=0)
            body(0, 1, done=1)
            with dve.Fori(0, B - 1) as b:
                body(b, 2)
                body(b, 3)
                body(b + 1, 0)
                body(b + 1, 1)
            body(B - 1, 2)
            body(B - 1, 3, last=True)
            reciprocals(B - 1, 2)
            for u in range(4):
                weighted_values(B - 1, 3, u)
            normalize(B - 1, 2)
            reciprocals(B - 1, 3)
            normalize(B - 1, 3)
            output(B - 1)
            add_output(B - 1)

        @block.scalar
        def _(act):
            def weights(b, q):
                j, slot = b * QUADS + q, q % 2
                """W = (eps + sqrt d2) ** -2 of a quad, as exp(-2 ln(eps + sqrt d2))."""
                for u in range(4):
                    act.wait_ge(s_d2, 2 * (j * 4 + u + 1))
                    nc.scalar.activation(w[:, slot, u, :, :], w[:, slot, u, :, :], ACT.Sqrt).then_inc(s_sqrt, 1)

                def ln(u):
                    act.wait_ge(s_sqrt, j * 4 + u + 1)
                    nc.scalar.activation(w[:, slot, u, :, :], w[:, slot, u, :, :], ACT.Ln, bias=ATT_EPS).then_inc(s_ln, 1)

                if q == 2 and not (isinstance(b, int) and b == B - 1):
                    root(nc, act, std[:, :], mv, b + 1, s_mv, s_std)
                nc.scalar.preload_act_table_set("natural_log_exp_and_others")
                ln(0)
                for u in range(4):
                    if u < 3:
                        ln(u + 1)
                    act.wait_ge(s_ln, j * 4 + u + 1)
                    nc.scalar.activation(w[:, slot, u, :, :], w[:, slot, u, :, :], ACT.Exp, scale=-2.0).then_inc(s_w, 1)

            root(nc, act, std[:, :], mv, 0, s_mv, s_std)
            with act.Fori(0, B - 1) as b:
                for q in range(QUADS):
                    weights(b, q)
            for q in range(QUADS):
                weights(B - 1, q)


def layernorm_stats(nc, dve, x, b, stats, mv, n, s_stats, s_mv, holder):
    nc.vector.memset(holder, 0.0)
    for c in range(NC):
        nc.vector.bn_stats(stats[:, c, :], chunk(x, b, c)).then_inc(s_stats, 1)
    dve.wait_ge(s_stats, NC * (n + 1))
    nc.vector.memset(holder, 0.0)
    for c in range(NC):
        nc.vector.bn_aggr(mv[:, c, :], stats[:, c, :]).then_inc(s_mv, 1)


def layernorm_apply(nc, dve, x, b, xn, mv, std, rstd, n, s_std, s_rstd, s_xn):
    dve.wait_ge(s_std, n + 1)
    nc.vector.reciprocal(rstd, std).then_inc(s_rstd, 1)
    dve.wait_ge(s_rstd, n + 1)
    for c in range(NC):
        nc.vector.tensor_scalar(xn[:, c, :], chunk(x, b, c), mv[:, c, 0:1], rstd[:, c:c + 1],
                                ALU.subtract, ALU.mult).then_inc(s_xn, 1)


def root(nc, act, std, mv, n, s_mv, s_std):
    act.wait_ge(s_mv, NC * (n + 1))
    nc.scalar.activation(std, mv[:, :, 1], ACT.Sqrt, bias=LN_EPS).then_inc(s_std, 1)


def chunk(x, b, c):
    return x[:, bass.ds(b * NC + c, 1), :].rearrange("p o d -> p (o d)")


def build_rest(nc, a, x1, out):
    with ExitStack() as ctx:
        def sb(name, shape, dt=F32):
            return ctx.enter_context(nc.sbuf_tensor(name, shape, dt))

        def psum(name, shape):
            return ctx.enter_context(nc.psum_tensor(name, shape, F32))

        x = sb("x", [P, B * NC, D])
        ident = sb("ident", [P, P])
        w1 = sb("w1", [P, NE, FF])
        w1s = [sb("w1_h", [P, NE, FF], F32R), sb("w1_l", [P, NE, FF], F32R)]
        w2 = sb("w2", [P, NE * NF, D])
        b1 = sb("b1", [P, NE * NF])
        b2 = sb("b2", [NE, D])
        wr = sb("wr", [P, NE])
        br = sb("br", [P, NE])
        wq = sb("wq", [P, D])
        bq = sb("bq", [P, 1])
        wkv = sb("wkv", [P, 2 * D])
        bkv = sb("bkv", [P, 2 * D])
        wo = sb("wo", [P, D])
        bo = sb("bo", [P, D])
        wrt = sb("wrt", [P, D])
        wblk = sb("wblk", [P, D])
        dec = sb("dec", [P, NC])
        hmask = sb("hmask", [P, D + H1])
        etri = sb("etri", [P, NE, NE])
        ttri = sb("ttri", [P, (2 * NC - 1) * P])
        holder = sb("holder2", [P, 1])

        stats_f = sb("stats_f", [P, NC, 6])
        mv_f = sb("mv_f", [P, NC, 2])
        std_f = sb("std_f", [P, NC])
        rstd_f = sb("rstd_f", [P, NC])
        xn_f = sb("xn_f", [P, NC, D])
        xT_f = sb("xT_f", [P, T])
        lg = sb("lg", [P, NC, NE])
        pr = sb("pr", [P, NC, NE])
        m4 = sb("m4", [P, NC])
        i4 = sb("i4", [P, NC])
        gt = sb("gt", [P, NC, NE, NE])
        eq = sb("eq", [P, NC, NE, NE])
        rank = sb("rank", [P, NC, NE])
        rw_next = sb("rw_next", [P, NC, NE])
        rw = sb("rw", [P, NC, NE])
        rwT = sb("rwT", [NE, T])
        xs = [sb("xs_h", [P, T], F32R), sb("xs_l", [P, T], F32R)]
        hr = sb("hr", [P, 2, T])
        hm = sb("hm", [P, 2, T])
        stats_t = sb("stats_t", [P, NC, 6])
        mv_t = sb("mv_t", [P, NC, 2])
        std_t = sb("std_t", [P, NC])
        rstd_t = sb("rstd_t", [P, NC])
        xn_t = sb("xn_t", [P, NC, D])
        xT_t = sb("xT_t", [P, T])
        yT = sb("yT", [P, T])
        qT = sb("qT", [P, T])
        kv = sb("kv", [P, NC, 2 * D + 1])
        kvm = sb("kvm", [P, D + H1])
        den = sb("den", [P, NC, H1])
        rden = sb("rden", [P, NC, H1])
        o1 = sb("o1", [P, NC, D])
        o1T = sb("o1T", [P, T])
        prod = sb("prod", [P, NC, D])
        score = sb("score", [P, NC])
        scr = sb("scr", [P, 2, NC, T])
        above = sb("above", [P, 2, NC])
        keep = sb("keep", [P, 2, NC])
        gel = sb("gel", [P, NC, D])
        res = sb("res", [P, NC, D])

        z = psum("z", [P, 2, T])
        y = psum("y", [P, T])
        rb = psum("rb", [P, 2, T])
        ta = psum("ta", [P, T])
        tb = psum("tb", [P, 2, T])

        names = """in_x in_rest_x in_front in_tail ones2 w1s chain_f chain_t
                 stats_f mv_f std_f rstd_f xn_f turn_f xT_f logits exp rw_next rwT_ps rwT xs rb z hr hm y yT yT_ps
                 stats_t mv_t std_t rstd_t xn_t turn_t xT_t qT_ps qT kv_ps kv kvm_ps kvm nd_ps o1 o1T_ps o1T y1_ps
                 score_col score_ps blk gel res out_dma""".split()
        S = {n: ctx.enter_context(nc.semaphore("s_" + n)) for n in names}
        in_w1 = [ctx.enter_context(nc.semaphore(f"s_in_w1_{e}")) for e in range(NE)]
        in_w2 = [ctx.enter_context(nc.semaphore(f"s_in_w2_{e}")) for e in range(NE)]
        NU = NE * NF
        front_loads = [
            (ident[:, :], a["c_ident"]), (wr[:, :], a["Wr"]), (br[:, :], a["br"].partition_broadcast(P)),
            (etri[:, :, :], a["c_etri"]), (b1[:, :], a["b1"]), (b2[:, :], a["b2"]),
        ]
        tail_loads = [
            (wq[:, :], a["W_q"]), (bq[:, :], a["b_q"].rearrange("(p o) -> p o", o=1)),
            (wkv[:, :], a["W_kv"]), (bkv[:, :], a["b_kv"].partition_broadcast(P)),
            (wo[:, :], a["W_o"]), (bo[:, :], a["b_o"].partition_broadcast(P)),
            (wrt[:, :], a["w_router"].partition_broadcast(P)), (wblk[:, :], a["w_block"]),
            (dec[:, :], a["c_dec"]), (hmask[:, :], a["c_hmask"]), (ttri[:, :], a["c_ttri"]),
        ]

        N_F = 13
        N_T = 13

        def over(t, n):
            t = t[tuple(slice(None) for _ in t.shape)]
            return t.unsqueeze(len(t.shape)).to_broadcast(list(t.shape) + [n])

        def every(t, n):
            t = t[tuple(slice(None) for _ in t.shape)]
            return t.unsqueeze(1).to_broadcast([t.shape[0], n] + list(t.shape[1:]))

        nat = "p (c d) -> p c d"
        block = ctx.enter_context(nc.Block())

        @block.sync
        def _(sp):
            sp.dma_start(x[:, 0:NC, :], x1[0]).then_inc(S["in_x"], 16)
            for dst, src in front_loads:
                sp.dma_start(dst, src).then_inc(S["in_front"], 16)
            for e in range(NE):
                sp.dma_start(w1[:, e, :], a["W1"][e]).then_inc(in_w1[e], 16)
                sp.dma_start(w2[:, e * NF:(e + 1) * NF, :], a["W2"][e].rearrange("(k p) d -> p k d", p=P)).then_inc(in_w2[e], 16)
            sp.dma_start(x[:, NC:, :].rearrange("p (b c) d -> p b c d", c=NC),
                         x1[1:].rearrange("b p c d -> p b c d")).then_inc(S["in_rest_x"], 16)
            for dst, src in tail_loads:
                sp.dma_start(dst, src).then_inc(S["in_tail"], 16)
            with sp.Fori(0, B) as b:
                sp.wait_ge(S["res"], b + 1)
                sp.dma_start(out[bass.ds(b, 1)].rearrange("o (c p) d -> p (o c) d", p=P), res[:, :, :]).then_inc(S["out_dma"], 16)
            sp.wait_ge(S["out_dma"], 16 * B + 1)

        @block.gpsimd
        def _(pool):
            nc.gpsimd.memset(kv[:, :, 2 * D:2 * D + 1], 1.0).then_inc(S["ones2"], 1)
            nc.gpsimd.memset(res[:, :, :], 0.0).then_inc(S["out_dma"], 1)

        @block.scalar
        def _(act):
            def root_f(f):
                root(nc, act, std_f[:, :], mv_f, f, S["mv_f"], S["std_f"])

            def turned_f(f):
                act.wait_ge(S["turn_f"], f + 1)
                nc.scalar.copy(xT_f[:, :], ta[:, :]).then_inc(S["xT_f"], 1)

            def exponential(f):
                act.wait_ge(S["chain_f"], N_F * f + 3)
                nc.scalar.activation(pr[:, :, :], lg[:, :, :], ACT.Exp).then_inc(S["exp"], 1)

            def turned_routing(f):
                act.wait_ge(S["rwT_ps"], f + 1)
                nc.scalar.copy(rwT[:, :], ta[0:NE, :]).then_inc(S["rwT"], 1)

            def experts_sum(t):
                act.wait_ge(S["y"], t + 1)
                nc.scalar.copy(yT[:, :], y[:, :]).then_inc(S["yT"], 1)

            def root_t(t, n):
                root(nc, act, std_t[:, :], mv_t, 2 * t + n, S["mv_t"], S["std_t"])

            def turned_t(t, n):
                act.wait_ge(S["turn_t"], 2 * t + n + 1)
                nc.scalar.copy(xT_t[:, :], ta[:, :]).then_inc(S["xT_t"], 1)

            def relu_q(t):
                act.wait_ge(S["qT_ps"], t + 1)
                nc.scalar.activation(qT[:, :], ta[:, :], ACT.Relu, bias=bq[:, 0:1]).then_inc(S["qT"], 1)

            def turned_o1(t):
                act.wait_ge(S["o1T_ps"], t + 1)
                nc.scalar.copy(o1T[:, :], ta[:, :]).then_inc(S["o1T"], 1)

            def gelu(t):
                act.wait_ge(S["blk"], t + 1)
                nc.scalar.activation(gel[:, :, :], tb[:, 0, :].rearrange(nat, c=NC), ACT.Gelu_apprx_tanh).then_inc(S["gel"], 1)

            def batch(b, tail=True, front=True):
                t, f = b - 1, b + 1
                for k in range(NU):
                    if tail:
                        if k == 0:
                            experts_sum(t)
                        if k == 2:
                            root_t(t, 0)
                        if k == 5:
                            turned_t(t, 0)
                        if k == 7:
                            relu_q(t)
                        if k == 16:
                            turned_o1(t)
                        if k == 19:
                            root_t(t, 1)
                        if k == 22:
                            turned_t(t, 1)
                        if k == 24:
                            gelu(t)
                    if front:
                        if k == 5:
                            root_f(f)
                        if k == 9:
                            turned_f(f)
                        if k == 14:
                            exponential(f)
                        if k == 20:
                            turned_routing(f)
                    n = b * NU + k
                    act.wait_ge(S["z"], n + 1)
                    if not isinstance(n, int) or n >= 2:
                        act.wait_ge(S["hm"], n - 1)
                    nc.scalar.activation(hr[:, k % 2, :], z[:, k % 2, :], ACT.Relu, bias=b1[:, k:k + 1]).then_inc(S["hr"], 1)

            root_f(0)
            turned_f(0)
            exponential(0)
            turned_routing(0)
            act.wait_ge(S["in_front"], 16 * len(front_loads))
            batch(0, tail=False)
            act.wait_ge(S["in_tail"], 16 * len(tail_loads))
            with act.Fori(1, B - 1) as b:
                batch(b)
            batch(B - 1, front=False)
            experts_sum(B - 1)
            root_t(B - 1, 0)
            turned_t(B - 1, 0)
            relu_q(B - 1)
            turned_o1(B - 1)
            root_t(B - 1, 1)
            turned_t(B - 1, 1)
            gelu(B - 1)

        @block.tensor
        def _(pe):
            def turn_f(f):
                pe.wait_ge(S["xn_f"], NC * (f + 1))
                for c in range(NC):
                    m = nc.tensor.transpose(ta[:, c * P:(c + 1) * P], xn_f[:, c, :], ident[:, :])
                m.then_inc(S["turn_f"], 1)

            def logits(f):
                pe.wait_ge(S["xT_f"], f + 1)
                for c in range(NC):
                    m = nc.tensor.matmul(ta[:, c * NE:(c + 1) * NE], xT_f[:, c * P:(c + 1) * P], wr[:, :],
                                         start=(c == 0), stop=True, skip_group_check=True)
                m.then_inc(S["logits"], 1)

            def turn_routing(f):
                pe.wait_ge(S["rw_next"], f + 1)
                for c in range(NC):
                    m = nc.tensor.transpose(ta[0:NE, c * P:(c + 1) * P], rw_next[:, c, :], ident[:, :])
                m.then_inc(S["rwT_ps"], 1)

            def turn_sum(t):
                pe.wait_ge(S["yT"], t + 1)
                for c in range(NC):
                    m = nc.tensor.transpose(ta[:, c * P:(c + 1) * P], yT[:, c * P:(c + 1) * P], ident[:, :])
                m.then_inc(S["yT_ps"], 1)

            def turn_t(t, n):
                pe.wait_ge(S["xn_t"], NC * (2 * t + n + 1))
                for c in range(NC):
                    m = nc.tensor.transpose(ta[:, c * P:(c + 1) * P], xn_t[:, c, :], ident[:, :])
                m.then_inc(S["turn_t"], 1)

            def qkv(t):
                pe.wait_ge(S["xT_t"], 2 * t + 1)
                nc.tensor.matmul(ta[:, :], wq[:, :], xT_t[:, :], start=True, stop=True).then_inc(S["qT_ps"], 1)
                for c in range(NC):
                    m = nc.tensor.matmul(tb[:, c // 2, (c % 2) * 2 * D:(c % 2 + 1) * 2 * D], xT_t[:, c * P:(c + 1) * P],
                                         wkv[:, :], start=(c % 2 == 0), stop=True, skip_group_check=True)
                m.then_inc(S["kv_ps"], 1)

            def keys_values(t):
                pe.wait_ge(S["kv"], t + 1)
                pe.wait_ge(S["qT"], t + 1)
                for c in range(NC):
                    m = nc.tensor.matmul(ta[:, 0:D + 1], kv[:, c, 0:D], kv[:, c, D:2 * D + 1], start=(c == 0), stop=(c == NC - 1))
                m.then_inc(S["kvm_ps"], 1)

            def numerators(t):
                pe.wait_ge(S["kvm"], t + 1)
                for c in range(NC):
                    m = nc.tensor.matmul(tb[:, c // 2, (c % 2) * 2 * D:(c % 2) * 2 * D + D + H1], qT[:, c * P:(c + 1) * P],
                                         kvm[:, :], start=(c % 2 == 0), stop=True, skip_group_check=True)
                m.then_inc(S["nd_ps"], 1)

            def turn_o1(t):
                pe.wait_ge(S["o1"], t + 1)
                for c in range(NC):
                    m = nc.tensor.transpose(ta[:, c * P:(c + 1) * P], o1[:, c, :], ident[:, :])
                m.then_inc(S["o1T_ps"], 1)

            def linear_output(t):
                pe.wait_ge(S["o1T"], t + 1)
                for c in range(NC):
                    m = nc.tensor.matmul(tb[:, 0, c * P:(c + 1) * P], o1T[:, c * P:(c + 1) * P], wo[:, :],
                                         start=(c == 0), stop=True, skip_group_check=True)
                m.then_inc(S["y1_ps"], 1)

            def scores(t):
                pe.wait_ge(S["score_col"], t + 1)
                for c in range(NC):
                    m = nc.tensor.transpose(tb[:, 1, c * P:(c + 1) * P], score[:, c:c + 1].to_broadcast([P, P]), ident[:, :])
                m.then_inc(S["score_ps"], 1)

            def processed(t):
                pe.wait_ge(S["xT_t"], 2 * t + 2)
                for c in range(NC):
                    m = nc.tensor.matmul(tb[:, 0, c * P:(c + 1) * P], xT_t[:, c * P:(c + 1) * P], wblk[:, :],
                                         start=(c == 0), stop=True, skip_group_check=True)
                m.then_inc(S["blk"], 1)

            def spread(b, e):
                if e >= 2:
                    pe.wait_ge(S["hm"], b * NU + (e - 1) * NF)
                for c in range(NC):
                    m = nc.tensor.transpose(rb[:, e % 2, c * P:(c + 1) * P],
                                            rw[:, c, e:e + 1].to_broadcast([P, P]), ident[:, :])
                m.then_inc(S["rb"], 1)

            def hidden(b, k):
                n = b * NU + k
                if k >= 2:
                    pe.wait_ge(S["hr"], n - 1)
                if isinstance(b, int) and b == 0 and k % NF == 0:
                    pe.wait_ge(S["w1s"], 2 * (k // NF) + 2)
                product(nc, z[:, k % 2, :], [w[:, k // NF, (k % NF) * P:(k % NF + 1) * P] for w in w1s],
                        [v[:, :] for v in xs]).then_inc(S["z"], 1)

            def batch(b, tail=True, front=True):
                t, f = b - 1, b + 1
                pe.wait_ge(S["xs"], 3 * b + 3)
                spread(b, 0)
                hidden(b, 0)
                hidden(b, 1)
                if tail:
                    pe.wait_ge(S["yT"], t + 1)
                pe.wait_ge(S["rwT"], b + 1)
                nc.tensor.matmul(y[:, :], b2[:, :], rwT[:, :], start=True, stop=False)
                for k in range(NU):
                    if tail:
                        if k == 0:
                            turn_sum(t)
                        if k == 4:
                            turn_t(t, 0)
                        if k == 6:
                            qkv(t)
                        if k == 10:
                            keys_values(t)
                        if k == 12:
                            numerators(t)
                        if k == 15:
                            turn_o1(t)
                        if k == 17:
                            linear_output(t)
                        if k == 21:
                            if front:
                                pe.wait_ge(S["rwT"], f + 1)
                            turn_t(t, 1)
                        if k == 22:
                            scores(t)
                        if k == 23:
                            processed(t)
                    if front:
                        if k == 8:
                            if tail:
                                pe.wait_ge(S["qT"], t + 1)
                            turn_f(f)
                        if k == 12:
                            logits(f)
                        if k == 19:
                            turn_routing(f)
                        if k == 9 and tail:
                            pe.wait_ge(S["xT_f"], f + 1)
                        if k == 14 and tail:
                            pe.wait_ge(S["chain_f"], N_F * f + 1)
                    if k % NF == 0 and k // NF + 1 < NE:
                        spread(b, k // NF + 1)
                    pe.wait_ge(S["hm"], b * NU + k + 1)
                    if isinstance(b, int) and b == 0 and k % NF == 0:
                        pe.wait_ge(in_w2[k // NF], 16)
                    m = nc.tensor.matmul(y[:, :], w2[:, k, :], hm[:, k % 2, :], start=False, stop=(k == NU - 1))
                    if k + 2 < NU:
                        hidden(b, k + 2)
                m.then_inc(S["y"], 1)

            pe.wait_ge(S["in_front"], 16 * len(front_loads))
            turn_f(0)
            logits(0)
            turn_routing(0)
            batch(0, tail=False)
            pe.wait_ge(S["in_tail"], 16 * len(tail_loads))
            with pe.Fori(1, B - 1) as b:
                batch(b)
            batch(B - 1, front=False)
            t = B - 1
            turn_sum(t)
            turn_t(t, 0)
            qkv(t)
            keys_values(t)
            numerators(t)
            turn_o1(t)
            linear_output(t)
            turn_t(t, 1)
            scores(t)
            processed(t)

        @block.vector
        def _(dve):
            V = nc.vector
            place = {}

            def link(chain, per_batch, b, ins):
                place[chain] = place.get(chain, 0) % per_batch + 1
                ins.then_inc(S[chain], 1)
                dve.wait_ge(S[chain], per_batch * b + place[chain])

            def front_stats(f):
                layernorm_stats(nc, dve, x, f, stats_f, mv_f, f, S["stats_f"], S["mv_f"], holder[:, :])

            def front_norm(f):
                layernorm_apply(nc, dve, x, f, xn_f, mv_f, std_f[:, :], rstd_f[:, :], f, S["std_f"], S["rstd_f"], S["xn_f"])

            def lf(f, ins):
                link("chain_f", N_F, f, ins)

            def lt(t, ins):
                link("chain_t", N_T, t, ins)

            def softmax_start(f):
                dve.wait_ge(S["logits"], f + 1)
                lf(f, V.tensor_tensor(lg[:, :, :], ta[:, 0:NC * NE].rearrange("p (c e) -> p c e", c=NC),
                                      every(br, NC), ALU.add))
                lf(f, V.tensor_reduce(m4[:, :], lg[:, :, :], AX.X, ALU.max))
                lf(f, V.tensor_tensor(lg[:, :, :], lg[:, :, :], over(m4, NE), ALU.subtract))

            def softmax_end(f):
                dve.wait_ge(S["exp"], f + 1)
                lf(f, V.tensor_reduce(m4[:, :], pr[:, :, :], AX.X, ALU.add))
                lf(f, V.reciprocal(i4[:, :], m4[:, :]))
                lf(f, V.tensor_tensor(pr[:, :, :], pr[:, :, :], over(i4, NE), ALU.mult))

            def expert_ranks(f):
                pj_ = pr[:, :, :].unsqueeze(2).to_broadcast([P, NC, NE, NE])
                pe_ = over(pr, NE)
                V.tensor_tensor(gt[:, :, :, :], pj_, pe_, ALU.is_gt)
                lf(f, V.tensor_tensor(eq[:, :, :, :], pj_, pe_, ALU.is_equal))
                lf(f, V.tensor_tensor(eq[:, :, :, :], eq[:, :, :, :], every(etri, NC), ALU.mult))
                lf(f, V.tensor_tensor(gt[:, :, :, :], gt[:, :, :, :], eq[:, :, :, :], ALU.add))

            def routing(f):
                lf(f, V.tensor_reduce(rank[:, :, :], gt[:, :, :, :], AX.X, ALU.add))
                lf(f, V.scalar_tensor_tensor(rw_next[:, :, :], rank[:, :, :], float(TOP_K), pr[:, :, :], ALU.is_lt, ALU.mult))
                lf(f, V.tensor_reduce(m4[:, :], rw_next[:, :, :], AX.X, ALU.add))
                lf(f, V.reciprocal(i4[:, :], m4[:, :]))
                V.tensor_tensor(rw_next[:, :, :], rw_next[:, :, :], over(i4, NE), ALU.mult).then_inc(S["rw_next"], 1)

            def hand_over(f):
                dve.wait_ge(S["xT_f"], f + 1)
                V.tensor_copy(xs[0][:, :], xT_f[:, :]).then_inc(S["xs"], 1)
                dve.wait_ge(S["rw_next"], f + 1)
                V.tensor_copy(rw[:, :, :], rw_next[:, :, :]).then_inc(S["xs"], 1)
                dve.wait_ge(S["xs"], 3 * f + 2)
                V.tensor_tensor(xs[1][:, :], xT_f[:, :], xs[0][:, :].bitcast(F32), ALU.subtract).then_inc(S["xs"], 1)

            def add_experts(t):
                dve.wait_ge(S["yT_ps"], t + 1)
                xc = x[:, bass.ds(t * NC, NC), :]
                lt(t, V.tensor_tensor(xc, xc, ta[:, :].rearrange(nat, c=NC), ALU.add))

            def tail_stats(t, n):
                layernorm_stats(nc, dve, x, t, stats_t, mv_t, 2 * t + n, S["stats_t"], S["mv_t"], holder[:, :])

            def tail_norm(t, n):
                layernorm_apply(nc, dve, x, t, xn_t, mv_t, std_t[:, :], rstd_t[:, :], 2 * t + n,
                                S["std_t"], S["rstd_t"], S["xn_t"])

            def add_kv_bias(t):
                dve.wait_ge(S["kv_ps"], t + 1)
                lt(t, V.tensor_tensor(kv[:, :, 0:2 * D], tb[:, :, :].rearrange("p g (c d) -> p (g c) d", c=2),
                                      every(bkv, NC), ALU.add))

            def decayed_keys(t):
                V.scalar_tensor_tensor(kv[:, :, 0:D], kv[:, :, 0:D], 0.0, over(dec, D), ALU.max, ALU.mult).then_inc(S["kv"], 1)

            def mask_heads(t):
                dve.wait_ge(S["kvm_ps"], t + 1)
                V.tensor_tensor(kvm[:, 0:D], ta[:, 0:D], hmask[:, 0:D], ALU.mult)
                V.tensor_scalar(kvm[:, D:D + H1], hmask[:, D:D + H1], ta[:, D:D + 1], None, ALU.mult).then_inc(S["kvm"], 1)

            nd = tb[:, :, :].rearrange("p g (c d) -> p (g c) d", c=2)

            def denominators(t):
                dve.wait_ge(S["nd_ps"], t + 1)
                lt(t, V.tensor_tensor(den[:, :, :], nd[:, :, D:D + H1], over(dec, H1), ALU.mult))
                lt(t, V.tensor_scalar(den[:, :, :], den[:, :, :], LIN_EPS, None, ALU.add))
                lt(t, V.reciprocal(rden[:, :, :], den[:, :, :]))
                lt(t, V.tensor_tensor(rden[:, :, :], rden[:, :, :], over(dec, H1), ALU.mult))

            def divide(t):
                V.tensor_tensor(o1[:, :, :].rearrange("p c (h e) -> p c h e", e=E1),
                                nd[:, :, 0:D].rearrange("p c (h e) -> p c h e", e=E1), over(rden, E1), ALU.mult).then_inc(S["o1"], 1)

            def add_linear(t):
                xc = x[:, bass.ds(t * NC, NC), :]
                dve.wait_ge(S["y1_ps"], t + 1)
                lt(t, V.tensor_tensor(prod[:, :, :], tb[:, 0, :].rearrange(nat, c=NC), every(bo, NC), ALU.add))
                lt(t, V.tensor_tensor(xc, xc, prod[:, :, :], ALU.add))

            def token_scores(t):
                dve.wait_ge(S["xn_t"], NC * (2 * t + 2))
                lt(t, V.tensor_tensor(prod[:, :, :], xn_t[:, :, :], every(wrt, NC), ALU.mult))
                V.tensor_reduce(score[:, :], prod[:, :, :], AX.X, ALU.add).then_inc(S["score_col"], 1)

            def token_ranks(t, c):
                dve.wait_ge(S["score_ps"], t + 1)
                V.tensor_scalar(scr[:, 0, c, :], tb[:, 1, :], score[:, c:c + 1], None, ALU.is_gt, ALU.add, accum_out=above[:, 0, c:c + 1])
                ins = V.scalar_tensor_tensor(scr[:, 1, c, :], tb[:, 1, :], score[:, c:c + 1],
                                             ttri[:, (NC - 1 - c) * P:(2 * NC - 1 - c) * P], ALU.is_equal, ALU.mult,
                                             accum_out=above[:, 1, c:c + 1])
                if c == NC - 1:
                    lt(t, ins)

            def kept(t):
                lt(t, V.tensor_tensor(above[:, 0, :], above[:, 0, :], above[:, 1, :], ALU.add))
                V.tensor_scalar(keep[:, 0, :], above[:, 0, :], float(KEEP), None, ALU.is_lt)
                lt(t, V.tensor_scalar(keep[:, 1, :], above[:, 0, :], float(KEEP), None, ALU.is_ge))

            def result_others(t):
                dve.wait_ge(S["out_dma"], 16 * t + 1)
                for c in range(NC):
                    ins = V.scalar_tensor_tensor(res[:, c, :], xn_t[:, c, :], keep[:, 1, c:c + 1], chunk(x, t, c), ALU.mult, ALU.add)
                lt(t, ins)

            def result_kept(t):
                dve.wait_ge(S["gel"], t + 1)
                for c in range(NC):
                    ins = V.scalar_tensor_tensor(res[:, c, :], gel[:, c, :], keep[:, 0, c:c + 1], res[:, c, :], ALU.mult, ALU.add)
                ins.then_inc(S["res"], 1)

            def split_w1(e):
                dve.wait_ge(in_w1[e], 16)
                V.tensor_copy(w1s[0][:, e, :], w1[:, e, :]).then_inc(S["w1s"], 1)
                dve.wait_ge(S["w1s"], 2 * e + 1)
                V.tensor_tensor(w1s[1][:, e, :], w1[:, e, :], w1s[0][:, e, :].bitcast(F32), ALU.subtract).then_inc(S["w1s"], 1)

            def batch(b, tail=True, front=True):
                t, f = b - 1, b + 1
                for k in range(NU):
                    if tail:
                        if k == 1:
                            add_experts(t)
                            tail_stats(t, 0)
                        if k == 3:
                            tail_norm(t, 0)
                        if k == 7:
                            add_kv_bias(t)
                        if k == 8:
                            decayed_keys(t)
                        if k == 11:
                            mask_heads(t)
                        if k == 13:
                            denominators(t)
                        if k == 14:
                            divide(t)
                        if k == 18:
                            add_linear(t)
                            tail_stats(t, 1)
                        if k == 20:
                            tail_norm(t, 1)
                        if k == 21:
                            token_scores(t)
                        if 23 <= k < 23 + NC:
                            token_ranks(t, k - 23)
                        if k == 27:
                            kept(t)
                        if k == 28:
                            result_others(t)
                        if k == 29:
                            result_kept(t)
                    if front:
                        if k == 4:
                            front_stats(f)
                        if k == 6:
                            front_norm(f)
                        if k == 13:
                            softmax_start(f)
                        if k == 15:
                            softmax_end(f)
                        if k == 16:
                            expert_ranks(f)
                        if k == 17:
                            routing(f)
                        if k == 31:
                            dve.wait_ge(S["z"], b * NU + NU)
                            hand_over(f)
                    if isinstance(b, int) and b == 0 and k % NF == 1 and k // NF + 2 < NE:
                        split_w1(k // NF + 2)
                    if isinstance(b, int) and b == 0 and k == 2:
                        dve.wait_ge(S["in_rest_x"], 16)
                    n = b * NU + k
                    if k % NF == 0:
                        dve.wait_ge(S["rb"], b * NE + k // NF + 1)
                    dve.wait_ge(S["hr"], n + 1)
                    V.tensor_tensor(hm[:, k % 2, :], hr[:, k % 2, :], rb[:, (k // NF) % 2, :], ALU.mult).then_inc(S["hm"], 1)

            dve.wait_ge(S["in_x"], 16)
            front_stats(0)
            front_norm(0)
            dve.wait_ge(S["in_front"], 16 * len(front_loads))
            softmax_start(0)
            softmax_end(0)
            expert_ranks(0)
            routing(0)
            hand_over(0)
            split_w1(0)
            split_w1(1)
            batch(0, tail=False)
            dve.wait_ge(S["in_tail"], 16 * len(tail_loads))
            dve.wait_ge(S["ones2"], 1)
            with dve.Fori(1, B - 1) as b:
                batch(b)
            batch(B - 1, front=False)
            t = B - 1
            add_experts(t)
            tail_stats(t, 0)
            tail_norm(t, 0)
            add_kv_bias(t)
            decayed_keys(t)
            mask_heads(t)
            denominators(t)
            divide(t)
            add_linear(t)
            tail_stats(t, 1)
            tail_norm(t, 1)
            token_scores(t)
            for c in range(NC):
                token_ranks(t, c)
            kept(t)
            result_others(t)
            result_kept(t)


def constants():
    f = np.float32
    nsel = np.zeros((P, 2, P), f)
    for i in range(2):
        for v in range(2):
            nsel[64 * v:64 * v + 64, i, 64 * i + 32 * v] = 1
    head = np.arange(D) // E1
    hmask = np.concatenate([head[:, None] == head[None, :], head[:, None] == np.arange(H1)[None, :]], 1).astype(f)
    e = np.arange(NE)
    etri = np.broadcast_to((e[None, :] < e[:, None]).astype(f), (P, NE, NE)).copy()
    j = np.arange((2 * NC - 1) * P) - (NC - 1) * P
    ttri = (j[None, :] < np.arange(P)[:, None]).astype(f)
    dec = np.exp(-np.arange(T, dtype=f) / f(T)).astype(f).reshape(NC, P).T.copy()
    return {"c_ident": np.eye(P, dtype=f), "c_nsel": nsel, "c_hmask": hmask, "c_etri": etri, "c_ttri": ttri, "c_dec": dec}


def kernel(**inputs):
    import concourse.bacc as _bacc
    from concourse.bass_utils import run_bass_kernel_spmd as _run

    i = {k: np.ascontiguousarray(v) for k, v in inputs.items()}
    win = i["L0_attn_W_in"].reshape(D, PAIRS, 2, 4, E0)
    bin_ = i["L0_attn_b_in"].reshape(PAIRS, 2, 4, E0)
    arrays = {
        "X": i["L0_attn_X"].reshape(B * T, D),
        "W_qkg": win[:, :, :, [0, 1, 3]].transpose(0, 1, 3, 2, 4).reshape(D, PAIRS, 3, P),
        "b_qkg": bin_[:, :, [0, 1, 3]].transpose(1, 3, 0, 2).reshape(P, PAIRS, 3),
        "W_v": win[:, :, :, 2].reshape(D, H0 * E0),
        "b_v": bin_[:, :, 2].reshape(H0 * E0),
        "W_out": i["L0_attn_W_out"], "b_out": i["L0_attn_b_out"],
        "W1": i["L0_ffn_W1"], "b1": i["L0_ffn_b1"].reshape(NE * NF, P).T,
        "W2": i["L0_ffn_W2"], "b2": i["L0_ffn_b2"], "Wr": i["L0_ffn_Wr"], "br": i["L0_ffn_br"],
        "W_q": i["L1_attn_W_q"].T, "b_q": i["L1_attn_b_q"],
        "W_kv": np.concatenate([i["L1_attn_W_k"].T, i["L1_attn_W_v"].T], 1),
        "b_kv": np.concatenate([i["L1_attn_b_k"], i["L1_attn_b_v"]]),
        "W_o": i["L1_attn_W_o"].T, "b_o": i["L1_attn_b_o"],
        "w_router": i["L1_ffn_w_router"], "w_block": i["L1_ffn_w_block"],
        **constants(),
    }
    arrays = {k: np.ascontiguousarray(v) for k, v in arrays.items()}
    nc = _bacc.Bacc("TRN2", target_bir_lowering=False, num_devices=1)
    a = {k: nc.dram_tensor(f"in_{k}", v.shape, F32, kind="ExternalInput").ap() for k, v in arrays.items()}
    out = nc.dram_tensor("out", (B, T, D), F32, kind="ExternalOutput").ap()
    build(nc, a, out)
    r = _run(nc, [{f"in_{k}": v for k, v in arrays.items()}], core_ids=[0])
    return r.results[0]["out"]
```

```python
from contextlib import ExitStack

import numpy as np

import concourse.bass as bass
from concourse import mybir

ALU = mybir.AluOpType
ACT = mybir.ActivationFunctionType
AX = mybir.AxisListType
F32 = mybir.dt.float32
F32R = mybir.dt.float32r

P = 128
B, T, D = 8, 512, 128
NC = T // P
H0, E0 = 16, 64
PAIRS = H0 // 2
QUADS = H0 // 4
ATT_EPS = 1e-4
LN_EPS = 1e-5
NE, FF = 8, 512
NF = FF // P
TOP_K = 2
H1, E1 = 16, 8
LIN_EPS = 1e-6
KEEP = T * 3 // 4

N_QKG, N_SUM, N_V, N_OUT, N_TURN = 6, 2, 2 * NC, 2, 2
N_BATCH = QUADS * (N_QKG + N_SUM) + N_V + N_OUT + N_TURN


def build(nc, a, out):
    def scratch(name, shape):
        return nc.dram_tensor(name, shape, F32, kind="Internal").ap()

    x1 = scratch("x1", (B, P, NC, D))
    dsum = scratch("head_sums", (QUADS, 2, 2, T))
    drec = scratch("head_recips", (QUADS, 2, 2, T))
    build_attention(nc, a, x1, dsum, drec)
    build_rest(nc, a, x1, out)


def product(nc, out, lhsT, rhs, start=True, stop=True):
    for i, (u, v) in enumerate(((0, 0), (1, 0), (0, 1))):
        m = nc.tensor.matmul(out, lhsT[u], rhs[v], start=start and i == 0, stop=stop and i == 2)
    return m


def build_attention(nc, a, x1, dsum, drec):
    with ExitStack() as ctx:
        def sb(name, shape, dt=F32):
            return ctx.enter_context(nc.sbuf_tensor(name, shape, dt))

        def psum(name, shape):
            return ctx.enter_context(nc.psum_tensor(name, shape, F32))

        def sem(name):
            return ctx.enter_context(nc.semaphore(name))

        xa = sb("xa", [P, NC, D])
        stats = sb("stats", [P, NC, 6])
        mv = sb("mv", [P, NC, 2])
        std = sb("std", [P, NC])
        rstd = sb("rstd", [P, NC])
        holder = sb("holder", [P, 1])
        xn = sb("xn", [P, NC, D])
        xs = [sb("xh", [P, T], F32R), sb("xl", [P, T], F32R)]
        wqkg = [sb("wqkg_h", [P, PAIRS, 3, P], F32R), sb("wqkg_l", [P, PAIRS, 3, P], F32R)]
        wv = [sb("wv_h", [P, H0 * E0], F32R), sb("wv_l", [P, H0 * E0], F32R)]
        wout = sb("wout", [P, PAIRS, D])
        bqkg = sb("bqkg", [P, PAIRS, 3])
        bv = sb("bv", [P, H0 * E0])
        bout = sb("bout", [P, 1])
        ident = sb("ident1", [P, P])
        nsel = sb("nsel", [P, 2, P])
        qk = sb("qk", [P, 2, T])
        sq = sb("sq", [P, 2, 2, T])
        query = sb("query", [P, 4, T])
        key = sb("key", [P, 4, T])
        gT = sb("gT", [P, PAIRS, T])
        hT = sb("hT", [P, PAIRS, T])
        vt = sb("vt", [P, NC, PAIRS, 3, E0])
        w = sb("w", [P, 2, 4, NC, T])
        srow = sb("srow", [P, 2, T])
        ssum = sb("ssum", [P, 2 * 2 * T // P])
        srec = sb("srec", [P, 2 * 2 * T // P])
        oT = sb("oT", [P, T])
        xc = sb("xc", [P, NC, D])

        pj = psum("pj", [P, 2, T])
        sc = psum("sc", [P, 2, 2, T])
        av = psum("av", [P, 2, T])

        s_w_in = sem("s_w_in")
        s_rest_in = sem("s_rest_in")
        s_rest_h = sem("s_rest_h")
        s_rest_l = sem("s_rest_l")
        s_in = sem("s_in")
        s_ident = sem("s_ident")
        s_wsplit = sem("s_wsplit")
        s_ones = sem("s_ones")
        s_xa = sem("s_xa")
        s_stats = sem("s_stats")
        s_mv = sem("s_mv")
        s_std = sem("s_std")
        s_rstd = sem("s_rstd")
        s_xn = sem("s_xn")
        s_xs = sem("s_xs")
        s_pj = sem("s_pj")
        s_pj_free = sem("s_pj_free")
        s_split = sem("s_split")
        s_sq = sem("s_sq")
        s_sc = sem("s_sc")
        s_d2 = sem("s_d2")
        s_sqrt = sem("s_sqrt")
        s_ln = sem("s_ln")
        s_w = sem("s_w")
        s_av = sem("s_av")
        s_av_free = sem("s_av_free")
        s_srow = sem("s_srow")
        s_sum_out = sem("s_sum_out")
        s_sum_in = sem("s_sum_in")
        s_sume = sem("s_sume")
        s_rec = sem("s_rec")
        s_rec_out = sem("s_rec_out")
        s_bc = sem("s_bc")
        s_hT = sem("s_hT")
        s_xc = sem("s_xc")
        s_x1_out = sem("s_x1_out")

        N_IN = 5

        def qkg_base(b, q):
            n = (0, N_QKG + N_SUM, 2 * (N_QKG + N_SUM) + N_V, 3 * (N_QKG + N_SUM) + N_V + N_OUT)[q]
            if isinstance(b, int) and b == 0 and q < 3:
                n += N_TURN
            return b * N_BATCH + n

        def use(b, q, i):
            late = q == 2 and i >= 4 and not (isinstance(b, int) and b == 0)
            return qkg_base(b, q) + i + (N_OUT if late else 0)

        def norm_base(b, q):
            between = 0
            if q == 2 and not (isinstance(b, int) and b == 0):
                between = N_OUT
            if q == 3 and not (isinstance(b, int) and b == B - 1):
                between = N_TURN
            return qkg_base(b, q) + N_QKG + between

        def v_base(b):
            return norm_base(b, 1) + N_SUM

        def out_base(b):
            if isinstance(b, int) and b == B - 1:
                return norm_base(b, 3) + N_SUM
            return qkg_base(b + 1, 2) + 4

        def turn_base(b):
            if isinstance(b, int) and b == 0:
                return 0
            return qkg_base(b - 1, 3) + N_QKG

        def weights_to_split():
            n, first = PAIRS * 3 * P, PAIRS * 3 * P // QUADS
            staged = w[:, 1].rearrange("p u c t -> p (u c t)")
            qkg = [m[:, :, :, :].rearrange("p g i e -> p (g i e)") for m in wqkg]
            return ((staged[:, 0:first], qkg[0][:, 0:first], qkg[1][:, 0:first]),
                    (staged[:, first:n], qkg[0][:, first:], qkg[1][:, first:]),
                    (staged[:, n:n + H0 * E0], wv[0][:, :], wv[1][:, :]))

        def later(b, q, n):
            return b + (q + n) // QUADS, (q + n) % QUADS

        block = ctx.enter_context(nc.Block())

        @block.sync
        def _(sp):
            X = a["X"].rearrange("(b c p) d -> b p c d", c=NC, p=P)

            def load_x(tile, b, sem):
                sp.dma_start(tile[:, :, :], X[bass.ds(b, 1)].rearrange("o p c d -> p (o c) d")).then_inc(sem, 16)

            load_x(xa, 0, s_xa)
            sp.dma_start(ident[:, :], a["c_ident"]).then_inc(s_ident, 16)
            n = PAIRS * 3 * P
            staged = w[:, 1].rearrange("p u c t -> p (u c t)")
            W = a["W_qkg"].rearrange("p g i e -> p (g i e)")
            sp.dma_start(staged[:, 0:n // QUADS], W[:, 0:n // QUADS]).then_inc(s_w_in, 16)
            sp.dma_start(bqkg[:, :, :], a["b_qkg"]).then_inc(s_in, 16)
            sp.dma_start(nsel[:, :, :], a["c_nsel"]).then_inc(s_in, 16)
            sp.dma_start(bv[:, :], a["b_v"].partition_broadcast(P)).then_inc(s_in, 16)
            sp.dma_start(wout[:, :, :], a["W_out"].rearrange("(g p) d -> p g d", p=P)).then_inc(s_in, 16)
            sp.dma_start(bout[:, :], a["b_out"].rearrange("(p o) -> p o", o=1)).then_inc(s_in, 16)
            sp.dma_start(staged[:, n // QUADS:n], W[:, n // QUADS:]).then_inc(s_rest_in, 16)
            sp.dma_start(staged[:, n:n + H0 * E0], a["W_v"]).then_inc(s_rest_in, 16)
            load_x(xc, 0, s_xc)

            def normalizer(b, q):
                j = b * QUADS + q
                sp.wait_ge(s_srow, 4 * (j + 1))
                sp.dma_start(dsum[q:q + 1, :, 0, :], srow[64:65, :, :]).then_inc(s_sum_out, 16)
                sp.dma_start(dsum[q:q + 1, :, 1, :], srow[0:1, :, :]).then_inc(s_sum_out, 16)
                sp.wait_ge(s_sum_out, 32 * (j + 1))
                sp.dma_start(ssum[:, :], dsum[q].rearrange("g v t -> (g v t)").rearrange("(p k) -> p k", p=P)).then_inc(s_sum_in, 16)
                sp.wait_ge(s_rec, j + 1)
                sp.dma_start(drec[q].rearrange("g v t -> (g v t)").rearrange("(p k) -> p k", p=P), srec[:, :]).then_inc(s_rec_out, 16)
                sp.wait_ge(s_rec_out, 16 * (j + 1))
                for v in range(2):
                    sp.dma_start(hT[64 * v:64 * v + 64, 2 * q:2 * q + 2, :],
                                 drec[q, :, v, :].partition_broadcast(64)).then_inc(s_bc, 16)

            def store_x1(b):
                sp.wait_ge(s_pj_free, out_base(b) + 2)
                sp.dma_start(x1[bass.ds(b, 1)].rearrange("o p c d -> p (o c) d"), xc[:, :, :]).then_inc(s_x1_out, 16)
                sp.wait_ge(s_x1_out, 16 * (b + 1))

            with sp.Fori(0, B - 1) as b:
                sp.wait_ge(s_xn, NC * (b + 1))
                load_x(xa, b + 1, s_xa)
                for q in range(QUADS):
                    normalizer(b, q)
                store_x1(b)
                load_x(xc, b + 1, s_xc)
            for q in range(QUADS):
                normalizer(B - 1, q)
            store_x1(B - 1)

        @block.gpsimd
        def _(pool):
            nc.gpsimd.memset(query[:, :, :], 0.0).then_inc(s_ones, 1)
            nc.gpsimd.memset(key[:, :, :], 0.0).then_inc(s_ones, 1)
            nc.gpsimd.memset(vt[:, :, :, 1, :], 1.0).then_inc(s_ones, 1)
            pool.wait_ge(s_ones, 3)
            nc.gpsimd.memset(query[96:97, :, :], 1.0).then_inc(s_ones, 1)
            pool.wait_ge(s_ones, 4)
            nc.gpsimd.memset(key[64:65, :, :], 1.0).then_inc(s_ones, 1)
            pool.wait_ge(s_ones, 5)

            def squares(b, q):
                for r in range(2):
                    for i in range(2):
                        pool.wait_ge(s_pj_free, use(b, q, 3 * r + i) + 1)
                        nc.gpsimd.tensor_tensor(sq[:, r, i, :], qk[:, i, :], qk[:, i, :], ALU.mult).then_inc(s_sq, 1)

            squares(0, 0)
            for k, (source, hi, lo) in enumerate(weights_to_split()[1:]):
                pool.wait_ge(s_rest_h, k + 1)
                nc.gpsimd.tensor_tensor(lo, source, hi.bitcast(F32), ALU.subtract).then_inc(s_rest_l, 1)
            squares(0, 1)
            squares(0, 2)
            with pool.Fori(0, B - 1) as b:
                squares(b, 3)
                for q in range(3):
                    squares(b + 1, q)
            squares(B - 1, 3)

        @block.tensor
        def _(pe):
            def bank_free(n):
                if not isinstance(n, int) or n >= 2:
                    pe.wait_ge(s_pj_free, n - 1)

            def turn(b):
                n = turn_base(b)
                pe.wait_ge(s_xn, NC * (b + 1))
                for h in range(2):
                    bank_free(n + h)
                    for c in range(2 * h, 2 * h + 2):
                        m = nc.tensor.transpose(pj[:, h, c % 2 * P:(c % 2 + 1) * P], xn[:, c, :], ident[:, :])
                    m.then_inc(s_pj, 1)

            def values(b):
                n = v_base(b)
                for c in range(NC):
                    for h in range(2):
                        bank_free(n + 2 * c + h)
                        product(nc, pj[:, h, :], [x[:, c * P:(c + 1) * P] for x in xs],
                                [v[:, h * T:(h + 1) * T] for v in wv]).then_inc(s_pj, 1)

            def projection(b, q, i):
                if q == 0 and i == 0:
                    pe.wait_ge(s_pj_free, turn_base(b) + 2)
                if isinstance(b, int) and (b, q, i) == (0, 1, 0):
                    pe.wait_ge(s_rest_l, 2)
                bank_free(use(b, q, i))
                product(nc, pj[:, i % 2, :], [m[:, 2 * q + i // 3, i % 3, :] for m in wqkg],
                        [x[:, :] for x in xs]).then_inc(s_pj, 1)

            def sums_of_squares(b, q):
                n = norm_base(b, q)
                for r in range(2):
                    g = (b * QUADS + q) * 2 + r
                    bank_free(n + r)
                    pe.wait_ge(s_sq, 2 * g + 2)
                    nc.tensor.matmul(pj[:, r, :], nsel[:, 0, :], sq[:, r, 0, :], start=True, stop=False)
                    nc.tensor.matmul(pj[:, r, :], nsel[:, 1, :], sq[:, r, 1, :],
                                     start=False, stop=True).then_inc(s_pj, 1)

            def distances(b, q):
                for u in range(4):
                    n = (b * QUADS + q) * 4 + u
                    pe.wait_ge(s_pj_free, norm_base(b, q) + 1 + u // 2)
                    for h in range(2):
                        if not isinstance(n, int) or n >= 1:
                            pe.wait_ge(s_d2, 2 * n + h - 1)
                        for k in range(2):
                            c = 2 * h + k
                            m = nc.tensor.matmul(sc[:, h, k, :], key[:, u, c * P:(c + 1) * P], query[:, u, :],
                                                 start=True, stop=True)
                        m.then_inc(s_sc, 1)

            def weighted_values(b, q, u):
                n = (b * QUADS + q) * 4 + u
                pe.wait_ge(s_w, n + 1)
                pe.wait_ge(s_av_free, n + 1)
                for c in range(NC):
                    lhsT = vt[:, c, 2 * q + u // 2, u % 2:u % 2 + 2, :].rearrange("p i e -> p (i e)")
                    m = nc.tensor.matmul(av[:, u % 2, :], lhsT, w[:, q % 2, u, c, :], start=(c == 0), stop=(c == NC - 1))
                m.then_inc(s_av, 1)

            def output(b):
                n = out_base(b)
                bank_free(n)
                for g in range(PAIRS):
                    if g % 2 == 0:
                        pe.wait_ge(s_hT, QUADS * b + g // 2 + 1)
                    m = nc.tensor.matmul(pj[:, 0, :], wout[:, g, :], hT[:, g, :], start=(g == 0), stop=(g == PAIRS - 1))
                m.then_inc(s_pj, 1)

            def turn_output(b):
                n = out_base(b)
                bank_free(n + 1)
                pe.wait_ge(s_pj_free, n + 1)
                for c in range(NC):
                    m = nc.tensor.transpose(pj[:, 1, c * P:(c + 1) * P], oT[:, c * P:(c + 1) * P], ident[:, :])
                m.then_inc(s_pj, 1)

            def body(b, q, first=False, last=False):
                next_quad, last_quad = later(b, q, 1), later(b, q, -1)
                ends = q == 1 and not (isinstance(b, int) and b == 0)
                distances(b, q)
                if not first:
                    weighted_values(*last_quad, 0)
                if not last:
                    projection(*next_quad, 0)
                    projection(*next_quad, 1)
                if not first:
                    weighted_values(*last_quad, 1)
                if not last:
                    projection(*next_quad, 2)
                    projection(*next_quad, 3)
                if ends:
                    output(b - 1)
                if not first:
                    weighted_values(*last_quad, 2)
                if ends:
                    turn_output(b - 1)
                if not last:
                    projection(*next_quad, 4)
                    projection(*next_quad, 5)
                if q == 2 and not (isinstance(b, int) and b == B - 1):
                    turn(b + 1)
                if not last and q != 2:
                    sums_of_squares(*next_quad)
                if not first:
                    weighted_values(*last_quad, 3)
                if q == 2:
                    sums_of_squares(*next_quad)
                if q == 0:
                    values(b)

            pe.wait_ge(s_ident, 16)
            turn(0)
            pe.wait_ge(s_wsplit, 2)
            for i in range(N_QKG):
                projection(0, 0, i)
            pe.wait_ge(s_in, 16 * N_IN)
            sums_of_squares(0, 0)
            body(0, 0, first=True)
            body(0, 1)
            with pe.Fori(0, B - 1) as b:
                body(b, 2)
                body(b, 3)
                body(b + 1, 0)
                body(b + 1, 1)
            body(B - 1, 2)
            body(B - 1, 3, last=True)
            for u in range(4):
                weighted_values(B - 1, 3, u)
            output(B - 1)
            turn_output(B - 1)

        @block.vector
        def _(dve):
            def bank_out(n):
                dve.wait_ge(s_pj, n + 1)

            def norm_stats(b):
                dve.wait_ge(s_xa, 16 * (b + 1))
                layernorm_stats(nc, dve, xa, 0, stats, mv, b, s_stats, s_mv, holder[:, :])

            def norm_apply(b):
                layernorm_apply(nc, dve, xa, 0, xn, mv, std[:, :], rstd[:, :], b, s_std, s_rstd, s_xn)

            def turned(b):
                n = turn_base(b)
                for h in range(2):
                    bank_out(n + h)
                    half = slice(h * T // 2, (h + 1) * T // 2)
                    nc.vector.tensor_copy(xs[0][:, half], pj[:, h, 0:T // 2]).then_inc(s_xs, 1)
                    dve.wait_ge(s_xs, 2 * b + h + 1)
                    nc.vector.tensor_tensor(xs[1][:, half], pj[:, h, 0:T // 2], xs[0][:, half].bitcast(F32),
                                            ALU.subtract).then_inc(s_pj_free, 1)

            def values(b):
                n = v_base(b)
                for c in range(NC):
                    for h in range(2):
                        bank_out(n + 2 * c + h)
                        heads = "p (g v e) -> p g v e"
                        nc.vector.tensor_tensor(vt[:, c, 4 * h:4 * h + 4, 0:3:2, :],
                                                pj[:, h, :].rearrange(heads, v=2, e=E0),
                                                bv[:, h * T:(h + 1) * T].rearrange(heads, v=2, e=E0),
                                                ALU.add).then_inc(s_pj_free, 1)

            def projection(b, q, i):
                j = b * QUADS + q
                r, part = i // 3, i % 3
                g = j * 2 + r
                bank_out(use(b, q, i))
                if part < 2:
                    if not isinstance(g, int) or g >= 1:
                        dve.wait_ge(s_sq, 2 * g + part - 1)
                        dve.wait_ge(s_split, 2 * g)
                    target = qk[:, part, :]
                else:
                    if q < 3 and (not isinstance(j, int) or j >= QUADS):
                        dve.wait_ge(s_hT, j - 3)
                    target = gT[:, 2 * q + r, :]
                nc.vector.tensor_scalar(target, pj[:, i % 2, :], bqkg[:, 2 * q + r, part:part + 1],
                                        None, ALU.add).then_inc(s_pj_free, 1)
                if i in (1, 5):
                    u = 2 * r
                    dve.wait_ge(s_pj_free, use(b, q, 3 * r + 1) + 1)
                    for v in range(2):
                        nc.vector.tensor_scalar(query[0:64, u + v, :], qk[64 * v:64 * v + 64, 0, :], -2.0, None, ALU.mult)
                        nc.vector.tensor_copy(key[0:64, u + v, :], qk[64 * v:64 * v + 64, 1, :]).then_inc(s_split, 1)

            def sums_of_squares(b, q):
                n = norm_base(b, q)
                for r in range(2):
                    u = 2 * r
                    bank_out(n + r)
                    for v in range(2):
                        nc.vector.tensor_copy(query[64:65, u + v, :], pj[32 * v:32 * v + 1, r, :])
                    nc.vector.tensor_copy(key[96:97, u, :], pj[64:65, r, :])
                    nc.vector.tensor_copy(key[96:97, u + 1, :], pj[96:97, r, :]).then_inc(s_pj_free, 1)

            def distances(b, q, u):
                for h in range(2):
                    n = ((b * QUADS + q) * 4 + u) * 2 + h
                    dve.wait_ge(s_sc, n + 1)
                    nc.vector.tensor_scalar(w[:, q % 2, u, 2 * h:2 * h + 2, :], sc[:, h, :, :], 0.0, None,
                                            ALU.max).then_inc(s_d2, 1)

            def weighted_values(b, q, u):
                j = b * QUADS + q
                n = j * 4 + u
                lo, row = (0, 64) if u % 2 == 0 else (64, 0)
                g = 2 * q + u // 2
                dve.wait_ge(s_av, n + 1)
                if u == 0 and (not isinstance(j, int) or j >= 1):
                    dve.wait_ge(s_sum_out, 32 * j)
                nc.vector.tensor_copy(srow[row:row + 1, u // 2, :], av[row:row + 1, u % 2, :]).then_inc(s_srow, 1)
                dve.wait_ge(s_pj_free, use(b, q, 3 * (u // 2) + 2) + 1)
                nc.vector.tensor_tensor(gT[lo:lo + 64, g, :], av[lo:lo + 64, u % 2, :], gT[lo:lo + 64, g, :],
                                        ALU.mult).then_inc(s_av_free, 1)

            def reciprocals(b, q):
                j = b * QUADS + q
                dve.wait_ge(s_sum_in, 16 * (j + 1))
                nc.vector.tensor_scalar(ssum[:, :], ssum[:, :], ATT_EPS, None, ALU.add).then_inc(s_sume, 1)
                dve.wait_ge(s_sume, j + 1)
                nc.vector.reciprocal(srec[:, :], ssum[:, :]).then_inc(s_rec, 1)

            def normalize(b, q):
                j = b * QUADS + q
                dve.wait_ge(s_bc, 32 * (j + 1))
                dve.wait_ge(s_av_free, 4 * (j + 1) + 2)
                nc.vector.tensor_tensor(hT[:, 2 * q:2 * q + 2, :], hT[:, 2 * q:2 * q + 2, :],
                                        gT[:, 2 * q:2 * q + 2, :], ALU.mult).then_inc(s_hT, 1)

            def output(b):
                n = out_base(b)
                bank_out(n)
                nc.vector.tensor_scalar(oT[:, :], pj[:, 0, :], bout[:, 0:1], None, ALU.add).then_inc(s_pj_free, 1)

            def add_output(b):
                n = out_base(b)
                bank_out(n + 1)
                dve.wait_ge(s_xc, 16 * (b + 1))
                nc.vector.tensor_tensor(xc[:, :, :], xc[:, :, :], pj[:, 1, :].rearrange("p (c d) -> p c d", c=NC),
                                        ALU.add).then_inc(s_pj_free, 1)

            def body(b, q, done=2, last=False):
                normed = q == 2 and not (isinstance(b, int) and b == B - 1)
                for u in range(3):
                    distances(b, q, u)
                if done >= 2:
                    reciprocals(*later(b, q, -2))
                if normed:
                    norm_stats(b + 1)
                distances(b, q, 3)
                next_quad, last_quad = later(b, q, 1), later(b, q, -1)
                ends = q == 1 and not (isinstance(b, int) and b == 0)
                if not last:
                    projection(*next_quad, 0)
                    projection(*next_quad, 1)
                if done >= 1:
                    weighted_values(*last_quad, 0)
                if done >= 2:
                    normalize(*later(b, q, -2))
                if not last:
                    projection(*next_quad, 2)
                    projection(*next_quad, 3)
                if done >= 1:
                    weighted_values(*last_quad, 1)
                if ends:
                    output(b - 1)
                if normed:
                    norm_apply(b + 1)
                if ends:
                    add_output(b - 1)
                if not last:
                    projection(*next_quad, 4)
                    projection(*next_quad, 5)
                if done >= 1:
                    weighted_values(*last_quad, 2)
                if normed:
                    turned(b + 1)
                if not last and q != 2:
                    sums_of_squares(*next_quad)
                if done >= 1:
                    weighted_values(*last_quad, 3)
                if q == 2:
                    sums_of_squares(*next_quad)
                if q == 0:
                    values(b)

            norm_stats(0)
            norm_apply(0)
            turned(0)
            source, hi, lo = weights_to_split()[0]
            dve.wait_ge(s_w_in, 16)
            nc.vector.tensor_copy(hi, source).then_inc(s_wsplit, 1)
            dve.wait_ge(s_wsplit, 1)
            nc.vector.tensor_tensor(lo, source, hi.bitcast(F32), ALU.subtract).then_inc(s_wsplit, 1)
            for u in range(2):
                nc.vector.memset(av[:, u, :], 0.0).then_inc(s_av_free, 1)
            dve.wait_ge(s_in, 16 * N_IN)
            dve.wait_ge(s_ones, 5)
            for i in range(N_QKG):
                projection(0, 0, i)
            sums_of_squares(0, 0)
            body(0, 0, done=0)
            body(0, 1, done=1)
            with dve.Fori(0, B - 1) as b:
                body(b, 2)
                body(b, 3)
                body(b + 1, 0)
                body(b + 1, 1)
            body(B - 1, 2)
            body(B - 1, 3, last=True)
            reciprocals(B - 1, 2)
            for u in range(4):
                weighted_values(B - 1, 3, u)
            normalize(B - 1, 2)
            reciprocals(B - 1, 3)
            normalize(B - 1, 3)
            output(B - 1)
            add_output(B - 1)

        @block.scalar
        def _(act):
            def weights(b, q):
                j, slot = b * QUADS + q, q % 2
                """W = (eps + sqrt d2) ** -2 of a quad, as exp(-2 ln(eps + sqrt d2))."""
                for u in range(4):
                    act.wait_ge(s_d2, 2 * (j * 4 + u + 1))
                    nc.scalar.activation(w[:, slot, u, :, :], w[:, slot, u, :, :], ACT.Sqrt).then_inc(s_sqrt, 1)

                def ln(u):
                    act.wait_ge(s_sqrt, j * 4 + u + 1)
                    nc.scalar.activation(w[:, slot, u, :, :], w[:, slot, u, :, :], ACT.Ln, bias=ATT_EPS).then_inc(s_ln, 1)

                if q == 2 and not (isinstance(b, int) and b == B - 1):
                    root(nc, act, std[:, :], mv, b + 1, s_mv, s_std)
                nc.scalar.preload_act_table_set("natural_log_exp_and_others")
                ln(0)
                for u in range(4):
                    if u < 3:
                        ln(u + 1)
                    act.wait_ge(s_ln, j * 4 + u + 1)
                    nc.scalar.activation(w[:, slot, u, :, :], w[:, slot, u, :, :], ACT.Exp, scale=-2.0).then_inc(s_w, 1)

            root(nc, act, std[:, :], mv, 0, s_mv, s_std)
            act.wait_ge(s_rest_in, 32)
            for source, hi, lo in weights_to_split()[1:]:
                nc.scalar.copy(hi, source).then_inc(s_rest_h, 1)
            with act.Fori(0, B - 1) as b:
                for q in range(QUADS):
                    weights(b, q)
            for q in range(QUADS):
                weights(B - 1, q)


def layernorm_stats(nc, dve, x, b, stats, mv, n, s_stats, s_mv, holder):
    nc.vector.memset(holder, 0.0)
    for c in range(NC):
        nc.vector.bn_stats(stats[:, c, :], chunk(x, b, c)).then_inc(s_stats, 1)
    dve.wait_ge(s_stats, NC * (n + 1))
    nc.vector.memset(holder, 0.0)
    for c in range(NC):
        nc.vector.bn_aggr(mv[:, c, :], stats[:, c, :]).then_inc(s_mv, 1)


def layernorm_apply(nc, dve, x, b, xn, mv, std, rstd, n, s_std, s_rstd, s_xn):
    dve.wait_ge(s_std, n + 1)
    nc.vector.reciprocal(rstd, std).then_inc(s_rstd, 1)
    dve.wait_ge(s_rstd, n + 1)
    for c in range(NC):
        nc.vector.tensor_scalar(xn[:, c, :], chunk(x, b, c), mv[:, c, 0:1], rstd[:, c:c + 1],
                                ALU.subtract, ALU.mult).then_inc(s_xn, 1)


def root(nc, act, std, mv, n, s_mv, s_std):
    act.wait_ge(s_mv, NC * (n + 1))
    nc.scalar.activation(std, mv[:, :, 1], ACT.Sqrt, bias=LN_EPS).then_inc(s_std, 1)


def chunk(x, b, c):
    return x[:, bass.ds(b * NC + c, 1), :].rearrange("p o d -> p (o d)")


def build_rest(nc, a, x1, out):
    with ExitStack() as ctx:
        def sb(name, shape, dt=F32):
            return ctx.enter_context(nc.sbuf_tensor(name, shape, dt))

        def psum(name, shape):
            return ctx.enter_context(nc.psum_tensor(name, shape, F32))

        x = sb("x", [P, B * NC, D])
        ident = sb("ident", [P, P])
        w1 = sb("w1", [P, NE, FF])
        w1s = [sb("w1_h", [P, NE, FF], F32R), sb("w1_l", [P, NE, FF], F32R)]
        w2 = sb("w2", [P, NE * NF, D])
        w2s = [sb("w2_h", [P, NE * NF, D], F32R), sb("w2_l", [P, NE * NF, D], F32R)]
        b1 = sb("b1", [P, NE * NF])
        b2 = sb("b2", [NE, D])
        wr = sb("wr", [P, NE])
        br = sb("br", [P, NE])
        wq = sb("wq", [P, D])
        bq = sb("bq", [P, 1])
        wkv = sb("wkv", [P, 2 * D])
        bkv = sb("bkv", [P, 2 * D])
        wo = sb("wo", [P, D])
        bo = sb("bo", [P, D])
        wrt = sb("wrt", [P, D])
        wblk = sb("wblk", [P, D])
        dec = sb("dec", [P, NC])
        hmask = sb("hmask", [P, D + H1])
        etri = sb("etri", [P, NE, NE])
        ttri = sb("ttri", [P, (2 * NC - 1) * P])
        holder = sb("holder2", [P, 1])

        stats_f = sb("stats_f", [P, NC, 6])
        mv_f = sb("mv_f", [P, NC, 2])
        std_f = sb("std_f", [P, NC])
        rstd_f = sb("rstd_f", [P, NC])
        xn_f = sb("xn_f", [P, NC, D])
        xT_f = sb("xT_f", [P, T])
        lg = sb("lg", [P, NC, NE])
        pr = sb("pr", [P, NC, NE])
        m4 = sb("m4", [P, NC])
        i4 = sb("i4", [P, NC])
        gt = sb("gt", [P, NC, NE, NE])
        eq = sb("eq", [P, NC, NE, NE])
        rank = sb("rank", [P, NC, NE])
        rw_next = sb("rw_next", [P, NC, NE])
        rw = sb("rw", [P, NC, NE])
        rwT = sb("rwT", [NE, T])
        xs = [sb("xs_h", [P, T], F32R), sb("xs_l", [P, T], F32R)]
        hr = sb("hr", [P, 2, T])
        hm = sb("hm", [P, 4, T])
        hms = [sb("hm_h", [P, 8, T], F32R), sb("hm_l", [P, 8, T], F32R)]
        stats_t = sb("stats_t", [P, NC, 6])
        mv_t = sb("mv_t", [P, NC, 2])
        std_t = sb("std_t", [P, NC])
        rstd_t = sb("rstd_t", [P, NC])
        xn_t = sb("xn_t", [P, NC, D])
        xT_t = sb("xT_t", [P, T])
        yT = sb("yT", [P, T])
        qT = sb("qT", [P, T])
        kv = sb("kv", [P, NC, 2 * D + 1])
        kvm = sb("kvm", [P, D + H1])
        den = sb("den", [P, NC, H1])
        rden = sb("rden", [P, NC, H1])
        o1 = sb("o1", [P, NC, D])
        o1T = sb("o1T", [P, T])
        prod = sb("prod", [P, NC, D])
        score = sb("score", [P, NC])
        scr = w1[:, :, :].rearrange("p (i c) t -> p i c t", i=2)
        above = sb("above", [P, 2, NC])
        keep = sb("keep", [P, 2, NC])
        gel = sb("gel", [P, NC, D])
        res = sb("res", [P, NC, D])

        z = psum("z", [P, 2, T])
        y = psum("y", [P, T])
        rb = psum("rb", [P, 2, T])
        ta = psum("ta", [P, T])
        tb = psum("tb", [P, 2, T])

        names = """in_x in_rest_x in_front in_tail ones2 w1s chain_f chain_t
                 stats_f mv_f std_f rstd_f xn_f turn_f xT_f logits exp rw_next rwT_ps rwT xs rb z hr hm hmh hml w2s y yT yT_ps
                 stats_t mv_t std_t rstd_t xn_t turn_t xT_t qT_ps qT kv_ps kv kvm_ps kvm nd_ps o1 o1T_ps o1T y1_ps
                 score_col score_ps blk gel res out_dma""".split()
        S = {n: ctx.enter_context(nc.semaphore("s_" + n)) for n in names}
        in_w1 = [ctx.enter_context(nc.semaphore(f"s_in_w1_{e}")) for e in range(NE)]
        in_w2 = [ctx.enter_context(nc.semaphore(f"s_in_w2_{e}")) for e in range(NE)]
        NU = NE * NF
        AHEAD = 5
        front_loads = [
            (ident[:, :], a["c_ident"]), (wr[:, :], a["Wr"]), (br[:, :], a["br"].partition_broadcast(P)),
            (etri[:, :, :], a["c_etri"]), (b1[:, :], a["b1"]), (b2[:, :], a["b2"]),
        ]
        tail_loads = [
            (wq[:, :], a["W_q"]), (bq[:, :], a["b_q"].rearrange("(p o) -> p o", o=1)),
            (wkv[:, :], a["W_kv"]), (bkv[:, :], a["b_kv"].partition_broadcast(P)),
            (wo[:, :], a["W_o"]), (bo[:, :], a["b_o"].partition_broadcast(P)),
            (wrt[:, :], a["w_router"].partition_broadcast(P)), (wblk[:, :], a["w_block"]),
            (dec[:, :], a["c_dec"]), (hmask[:, :], a["c_hmask"]), (ttri[:, :], a["c_ttri"]),
        ]

        N_F = 13
        N_T = 13

        def over(t, n):
            t = t[tuple(slice(None) for _ in t.shape)]
            return t.unsqueeze(len(t.shape)).to_broadcast(list(t.shape) + [n])

        def every(t, n):
            t = t[tuple(slice(None) for _ in t.shape)]
            return t.unsqueeze(1).to_broadcast([t.shape[0], n] + list(t.shape[1:]))

        nat = "p (c d) -> p c d"
        lg_ps = tb[:, 1, T - NC * NE:T]
        block = ctx.enter_context(nc.Block())

        @block.sync
        def _(sp):
            sp.dma_start(x[:, 0:NC, :], x1[0]).then_inc(S["in_x"], 16)
            for dst, src in front_loads:
                sp.dma_start(dst, src).then_inc(S["in_front"], 16)
            for e in range(NE):
                sp.dma_start(w1[:, e, :], a["W1"][e]).then_inc(in_w1[e], 16)
                sp.dma_start(w2[:, e * NF:(e + 1) * NF, :], a["W2"][e].rearrange("(k p) d -> p k d", p=P)).then_inc(in_w2[e], 16)
            sp.dma_start(x[:, NC:, :].rearrange("p (b c) d -> p b c d", c=NC),
                         x1[1:].rearrange("b p c d -> p b c d")).then_inc(S["in_rest_x"], 16)
            for dst, src in tail_loads:
                sp.dma_start(dst, src).then_inc(S["in_tail"], 16)
            with sp.Fori(0, B) as b:
                sp.wait_ge(S["res"], b + 1)
                sp.dma_start(out[bass.ds(b, 1)].rearrange("o (c p) d -> p (o c) d", p=P), res[:, :, :]).then_inc(S["out_dma"], 16)
            sp.wait_ge(S["out_dma"], 16 * B + 1)

        @block.gpsimd
        def _(pool):
            nc.gpsimd.memset(kv[:, :, 2 * D:2 * D + 1], 1.0).then_inc(S["ones2"], 1)
            nc.gpsimd.memset(res[:, :, :], 0.0).then_inc(S["out_dma"], 1)

            def split_w2(e):
                experts = slice(e * NF, (e + 1) * NF)
                pool.wait_ge(in_w2[e], 16)
                nc.gpsimd.tensor_copy(w2s[0][:, experts, :], w2[:, experts, :]).then_inc(S["w2s"], 1)
                pool.wait_ge(S["w2s"], 2 * e + 1)
                nc.gpsimd.tensor_tensor(w2s[1][:, experts, :], w2[:, experts, :], w2s[0][:, experts, :].bitcast(F32),
                                        ALU.subtract).then_inc(S["w2s"], 1)

            def low_parts(b):
                for k in range(NU):
                    if isinstance(b, int) and b == 0 and k % NF == 1 and k // NF + 2 < NE:
                        split_w2(k // NF + 2)
                    pool.wait_ge(S["hmh"], b * NU + k + 1)
                    nc.gpsimd.tensor_tensor(hms[1][:, k % 8, :], hm[:, k % 4, :], hms[0][:, k % 8, :].bitcast(F32),
                                            ALU.subtract).then_inc(S["hml"], 1)

            split_w2(0)
            split_w2(1)
            low_parts(0)
            with pool.Fori(1, B) as b:
                low_parts(b)

        @block.scalar
        def _(act):
            def root_f(f):
                root(nc, act, std_f[:, :], mv_f, f, S["mv_f"], S["std_f"])

            def turned_f(f):
                act.wait_ge(S["turn_f"], f + 1)
                nc.scalar.copy(xT_f[:, :], ta[:, :]).then_inc(S["xT_f"], 1)

            def exponential(f):
                act.wait_ge(S["chain_f"], N_F * f + 3)
                nc.scalar.activation(pr[:, :, :], lg[:, :, :], ACT.Exp).then_inc(S["exp"], 1)

            def turned_routing(f):
                act.wait_ge(S["rwT_ps"], f + 1)
                nc.scalar.copy(rwT[:, :], ta[0:NE, :]).then_inc(S["rwT"], 1)

            def experts_sum(t):
                act.wait_ge(S["y"], t + 1)
                nc.scalar.copy(yT[:, :], y[:, :]).then_inc(S["yT"], 1)

            def root_t(t, n):
                root(nc, act, std_t[:, :], mv_t, 2 * t + n, S["mv_t"], S["std_t"])

            def turned_t(t, n):
                act.wait_ge(S["turn_t"], 2 * t + n + 1)
                nc.scalar.copy(xT_t[:, :], ta[:, :]).then_inc(S["xT_t"], 1)

            def relu_q(t):
                act.wait_ge(S["qT_ps"], t + 1)
                nc.scalar.activation(qT[:, :], ta[:, :], ACT.Relu, bias=bq[:, 0:1]).then_inc(S["qT"], 1)

            def turned_o1(t):
                act.wait_ge(S["o1T_ps"], t + 1)
                nc.scalar.copy(o1T[:, :], ta[:, :]).then_inc(S["o1T"], 1)

            def gelu(t):
                act.wait_ge(S["blk"], t + 1)
                nc.scalar.activation(gel[:, :, :], tb[:, 0, :].rearrange(nat, c=NC), ACT.Gelu_apprx_tanh).then_inc(S["gel"], 1)

            def high_part(b, k):
                act.wait_ge(S["hm"], b * NU + k + 1)
                nc.scalar.copy(hms[0][:, k % 8, :], hm[:, k % 4, :]).then_inc(S["hmh"], 1)

            def batch(b, tail=True, front=True):
                t, f = b - 1, b + 1
                for k in range(NU):
                    if tail:
                        if k == 4:
                            experts_sum(t)
                        if k == 6:
                            root_t(t, 0)
                        if k == 10:
                            turned_t(t, 0)
                        if k == 12:
                            relu_q(t)
                        if k == 20:
                            turned_o1(t)
                        if k == 23:
                            root_t(t, 1)
                        if k == 26:
                            turned_t(t, 1)
                        if k == 28:
                            gelu(t)
                    if front:
                        if k == 9:
                            root_f(f)
                        if k == 14:
                            turned_f(f)
                        if k == 17:
                            exponential(f)
                        if k == 23:
                            turned_routing(f)
                    n = b * NU + k
                    act.wait_ge(S["z"], n + 1)
                    if not isinstance(n, int) or n >= 2:
                        act.wait_ge(S["hm"], n - 1)
                    nc.scalar.activation(hr[:, k % 2, :], z[:, k % 2, :], ACT.Relu, bias=b1[:, k:k + 1]).then_inc(S["hr"], 1)
                    if k >= 1:
                        high_part(b, k - 1)
                high_part(b, NU - 1)

            root_f(0)
            turned_f(0)
            exponential(0)
            turned_routing(0)
            act.wait_ge(S["in_front"], 16 * len(front_loads))
            batch(0, tail=False)
            act.wait_ge(S["in_tail"], 16 * len(tail_loads))
            with act.Fori(1, B - 1) as b:
                batch(b)
            batch(B - 1, front=False)
            experts_sum(B - 1)
            root_t(B - 1, 0)
            turned_t(B - 1, 0)
            relu_q(B - 1)
            turned_o1(B - 1)
            root_t(B - 1, 1)
            turned_t(B - 1, 1)
            gelu(B - 1)

        @block.tensor
        def _(pe):
            def turn_f(f):
                pe.wait_ge(S["xn_f"], NC * (f + 1))
                for c in range(NC):
                    m = nc.tensor.transpose(ta[:, c * P:(c + 1) * P], xn_f[:, c, :], ident[:, :])
                m.then_inc(S["turn_f"], 1)

            def logits(f):
                pe.wait_ge(S["xT_f"], f + 1)
                for c in range(NC):
                    m = nc.tensor.matmul(lg_ps[:, c * NE:(c + 1) * NE], xT_f[:, c * P:(c + 1) * P], wr[:, :],
                                         start=(c == 0), stop=True, skip_group_check=True)
                m.then_inc(S["logits"], 1)

            def turn_routing(f):
                pe.wait_ge(S["rw_next"], f + 1)
                for c in range(NC):
                    m = nc.tensor.transpose(ta[0:NE, c * P:(c + 1) * P], rw_next[:, c, :], ident[:, :])
                m.then_inc(S["rwT_ps"], 1)

            def turn_sum(t):
                pe.wait_ge(S["yT"], t + 1)
                for c in range(NC):
                    m = nc.tensor.transpose(ta[:, c * P:(c + 1) * P], yT[:, c * P:(c + 1) * P], ident[:, :])
                m.then_inc(S["yT_ps"], 1)

            def turn_t(t, n):
                pe.wait_ge(S["xn_t"], NC * (2 * t + n + 1))
                for c in range(NC):
                    m = nc.tensor.transpose(ta[:, c * P:(c + 1) * P], xn_t[:, c, :], ident[:, :])
                m.then_inc(S["turn_t"], 1)

            def qkv(t):
                pe.wait_ge(S["xT_t"], 2 * t + 1)
                nc.tensor.matmul(ta[:, :], wq[:, :], xT_t[:, :], start=True, stop=True).then_inc(S["qT_ps"], 1)
                for c in range(NC):
                    m = nc.tensor.matmul(tb[:, c // 2, (c % 2) * 2 * D:(c % 2 + 1) * 2 * D], xT_t[:, c * P:(c + 1) * P],
                                         wkv[:, :], start=(c % 2 == 0), stop=True, skip_group_check=True)
                m.then_inc(S["kv_ps"], 1)

            def keys_values(t):
                pe.wait_ge(S["kv"], t + 1)
                pe.wait_ge(S["qT"], t + 1)
                for c in range(NC):
                    m = nc.tensor.matmul(ta[:, 0:D + 1], kv[:, c, 0:D], kv[:, c, D:2 * D + 1], start=(c == 0), stop=(c == NC - 1))
                m.then_inc(S["kvm_ps"], 1)

            def numerators(t):
                pe.wait_ge(S["kvm"], t + 1)
                for c in range(NC):
                    m = nc.tensor.matmul(tb[:, c // 2, (c % 2) * 2 * D:(c % 2) * 2 * D + D + H1], qT[:, c * P:(c + 1) * P],
                                         kvm[:, :], start=(c % 2 == 0), stop=True, skip_group_check=True)
                m.then_inc(S["nd_ps"], 1)

            def turn_o1(t):
                pe.wait_ge(S["o1"], t + 1)
                for c in range(NC):
                    m = nc.tensor.transpose(ta[:, c * P:(c + 1) * P], o1[:, c, :], ident[:, :])
                m.then_inc(S["o1T_ps"], 1)

            def linear_output(t):
                pe.wait_ge(S["o1T"], t + 1)
                for c in range(NC):
                    m = nc.tensor.matmul(tb[:, 0, c * P:(c + 1) * P], o1T[:, c * P:(c + 1) * P], wo[:, :],
                                         start=(c == 0), stop=True, skip_group_check=True)
                m.then_inc(S["y1_ps"], 1)

            def scores(t):
                pe.wait_ge(S["score_col"], t + 1)
                for c in range(NC):
                    m = nc.tensor.transpose(tb[:, 1, c * P:(c + 1) * P], score[:, c:c + 1].to_broadcast([P, P]), ident[:, :])
                m.then_inc(S["score_ps"], 1)

            def processed(t):
                pe.wait_ge(S["xT_t"], 2 * t + 2)
                for c in range(NC):
                    m = nc.tensor.matmul(tb[:, 0, c * P:(c + 1) * P], xT_t[:, c * P:(c + 1) * P], wblk[:, :],
                                         start=(c == 0), stop=True, skip_group_check=True)
                m.then_inc(S["blk"], 1)

            def spread(b, e):
                if e >= 2:
                    pe.wait_ge(S["hm"], b * NU + (e - 1) * NF)
                elif not isinstance(b, int) or b >= 1:
                    pe.wait_ge(S["hm"], b * NU + (e - 1) * NF)
                for c in range(NC):
                    m = nc.tensor.transpose(rb[:, e % 2, c * P:(c + 1) * P],
                                            rw[:, c, e:e + 1].to_broadcast([P, P]), ident[:, :])
                m.then_inc(S["rb"], 1)

            def hidden(b, k):
                n = b * NU + k
                if not isinstance(n, int) or n >= 2:
                    pe.wait_ge(S["hr"], n - 1)
                if isinstance(b, int) and b == 0 and k % NF == 0:
                    pe.wait_ge(S["w1s"], 2 * (k // NF) + 2)
                product(nc, z[:, k % 2, :], [w[:, k // NF, (k % NF) * P:(k % NF + 1) * P] for w in w1s],
                        [v[:, :] for v in xs]).then_inc(S["z"], 1)

            def batch(b, tail=True, front=True):
                t, f = b - 1, b + 1
                if tail:
                    pe.wait_ge(S["yT"], t + 1)
                pe.wait_ge(S["rwT"], b + 1)
                nc.tensor.matmul(y[:, :], b2[:, :], rwT[:, :], start=True, stop=False)
                for k in range(NU):
                    if tail:
                        if k == 0:
                            turn_sum(t)
                        if k == 5:
                            turn_t(t, 0)
                        if k == 7:
                            if not isinstance(t, int) or t >= 1:
                                pe.wait_ge(S["chain_t"], N_T * t)
                            qkv(t)
                        if k == 11:
                            if front:
                                pe.wait_ge(S["xT_f"], f + 1)
                            keys_values(t)
                        if k == 13:
                            if front:
                                pe.wait_ge(S["chain_f"], N_F * f + 1)
                            numerators(t)
                        if k == 16:
                            turn_o1(t)
                        if k == 17:
                            linear_output(t)
                        if k == 22:
                            if front:
                                pe.wait_ge(S["rwT"], f + 1)
                            turn_t(t, 1)
                        if k == 23:
                            scores(t)
                        if k == 23:
                            processed(t)
                    if front:
                        if k == 9:
                            if tail:
                                pe.wait_ge(S["qT"], t + 1)
                            turn_f(f)
                        if k == 11:
                            logits(f)
                        if k == 18:
                            turn_routing(f)
                        if k == 28:
                            spread(f, 0)
                        if k == 30:
                            spread(f, 1)
                    if k % NF == 1 and k // NF + 2 < NE:
                        spread(b, k // NF + 2)
                    if isinstance(b, int) and b == 0 and k % NF == 0:
                        pe.wait_ge(S["w2s"], 2 * (k // NF) + 2)
                    pe.wait_ge(S["hml"], b * NU + k + 1)
                    m = product(nc, y[:, :], [w[:, k, :] for w in w2s], [v[:, k % 8, :] for v in hms],
                                start=False, stop=(k == NU - 1))
                    if k == NU - 1:
                        m.then_inc(S["y"], 1)
                    if k + AHEAD < NU:
                        hidden(b, k + AHEAD)
                    elif front:
                        if k + AHEAD == NU:
                            pe.wait_ge(S["xs"], 3 * f + 3)
                        hidden(f, k + AHEAD - NU)

            pe.wait_ge(S["in_front"], 16 * len(front_loads))
            turn_f(0)
            logits(0)
            turn_routing(0)
            pe.wait_ge(S["xs"], 3)
            spread(0, 0)
            spread(0, 1)
            for k in range(AHEAD):
                hidden(0, k)
            batch(0, tail=False)
            pe.wait_ge(S["in_tail"], 16 * len(tail_loads))
            batch(1)
            with pe.Fori(2, B - 1) as b:
                batch(b)
            batch(B - 1, front=False)
            t = B - 1
            turn_sum(t)
            turn_t(t, 0)
            pe.wait_ge(S["chain_t"], N_T * t)
            qkv(t)
            keys_values(t)
            numerators(t)
            turn_o1(t)
            linear_output(t)
            turn_t(t, 1)
            scores(t)
            processed(t)

        @block.vector
        def _(dve):
            V = nc.vector
            place = {}

            def link(chain, per_batch, b, ins):
                place[chain] = place.get(chain, 0) % per_batch + 1
                ins.then_inc(S[chain], 1)
                dve.wait_ge(S[chain], per_batch * b + place[chain])

            def front_stats(f):
                layernorm_stats(nc, dve, x, f, stats_f, mv_f, f, S["stats_f"], S["mv_f"], holder[:, :])

            def front_norm(f):
                layernorm_apply(nc, dve, x, f, xn_f, mv_f, std_f[:, :], rstd_f[:, :], f, S["std_f"], S["rstd_f"], S["xn_f"])

            def lf(f, ins):
                link("chain_f", N_F, f, ins)

            def lt(t, ins):
                link("chain_t", N_T, t, ins)

            def softmax_start(f):
                dve.wait_ge(S["logits"], f + 1)
                lf(f, V.tensor_tensor(lg[:, :, :], lg_ps.rearrange("p (c e) -> p c e", c=NC),
                                      every(br, NC), ALU.add))
                lf(f, V.tensor_reduce(m4[:, :], lg[:, :, :], AX.X, ALU.max))
                lf(f, V.tensor_tensor(lg[:, :, :], lg[:, :, :], over(m4, NE), ALU.subtract))

            def softmax_end(f):
                dve.wait_ge(S["exp"], f + 1)
                lf(f, V.tensor_reduce(m4[:, :], pr[:, :, :], AX.X, ALU.add))
                lf(f, V.reciprocal(i4[:, :], m4[:, :]))
                lf(f, V.tensor_tensor(pr[:, :, :], pr[:, :, :], over(i4, NE), ALU.mult))

            def expert_ranks(f):
                pj_ = pr[:, :, :].unsqueeze(2).to_broadcast([P, NC, NE, NE])
                pe_ = over(pr, NE)
                V.tensor_tensor(gt[:, :, :, :], pj_, pe_, ALU.is_gt)
                lf(f, V.tensor_tensor(eq[:, :, :, :], pj_, pe_, ALU.is_equal))
                lf(f, V.tensor_tensor(eq[:, :, :, :], eq[:, :, :, :], every(etri, NC), ALU.mult))
                lf(f, V.tensor_tensor(gt[:, :, :, :], gt[:, :, :, :], eq[:, :, :, :], ALU.add))

            def routing(f):
                lf(f, V.tensor_reduce(rank[:, :, :], gt[:, :, :, :], AX.X, ALU.add))
                lf(f, V.scalar_tensor_tensor(rw_next[:, :, :], rank[:, :, :], float(TOP_K), pr[:, :, :], ALU.is_lt, ALU.mult))
                lf(f, V.tensor_reduce(m4[:, :], rw_next[:, :, :], AX.X, ALU.add))
                lf(f, V.reciprocal(i4[:, :], m4[:, :]))
                V.tensor_tensor(rw_next[:, :, :], rw_next[:, :, :], over(i4, NE), ALU.mult).then_inc(S["rw_next"], 1)

            def hand_over(f):
                dve.wait_ge(S["xT_f"], f + 1)
                V.tensor_copy(xs[0][:, :], xT_f[:, :]).then_inc(S["xs"], 1)
                dve.wait_ge(S["rw_next"], f + 1)
                V.tensor_copy(rw[:, :, :], rw_next[:, :, :]).then_inc(S["xs"], 1)
                dve.wait_ge(S["xs"], 3 * f + 2)
                V.tensor_tensor(xs[1][:, :], xT_f[:, :], xs[0][:, :].bitcast(F32), ALU.subtract).then_inc(S["xs"], 1)

            def add_experts(t):
                dve.wait_ge(S["yT_ps"], t + 1)
                xc = x[:, bass.ds(t * NC, NC), :]
                lt(t, V.tensor_tensor(xc, xc, ta[:, :].rearrange(nat, c=NC), ALU.add))

            def tail_stats(t, n):
                layernorm_stats(nc, dve, x, t, stats_t, mv_t, 2 * t + n, S["stats_t"], S["mv_t"], holder[:, :])

            def tail_norm(t, n):
                layernorm_apply(nc, dve, x, t, xn_t, mv_t, std_t[:, :], rstd_t[:, :], 2 * t + n,
                                S["std_t"], S["rstd_t"], S["xn_t"])

            def add_kv_bias(t):
                dve.wait_ge(S["kv_ps"], t + 1)
                lt(t, V.tensor_tensor(kv[:, :, 0:2 * D], tb[:, :, :].rearrange("p g (c d) -> p (g c) d", c=2),
                                      every(bkv, NC), ALU.add))

            def decayed_keys(t):
                V.scalar_tensor_tensor(kv[:, :, 0:D], kv[:, :, 0:D], 0.0, over(dec, D), ALU.max, ALU.mult).then_inc(S["kv"], 1)

            def mask_heads(t):
                dve.wait_ge(S["kvm_ps"], t + 1)
                V.tensor_tensor(kvm[:, 0:D], ta[:, 0:D], hmask[:, 0:D], ALU.mult)
                V.tensor_scalar(kvm[:, D:D + H1], hmask[:, D:D + H1], ta[:, D:D + 1], None, ALU.mult).then_inc(S["kvm"], 1)

            nd = tb[:, :, :].rearrange("p g (c d) -> p (g c) d", c=2)

            def denominators(t):
                dve.wait_ge(S["nd_ps"], t + 1)
                lt(t, V.tensor_tensor(den[:, :, :], nd[:, :, D:D + H1], over(dec, H1), ALU.mult))
                lt(t, V.tensor_scalar(den[:, :, :], den[:, :, :], LIN_EPS, None, ALU.add))
                lt(t, V.reciprocal(rden[:, :, :], den[:, :, :]))
                lt(t, V.tensor_tensor(rden[:, :, :], rden[:, :, :], over(dec, H1), ALU.mult))

            def divide(t):
                V.tensor_tensor(o1[:, :, :].rearrange("p c (h e) -> p c h e", e=E1),
                                nd[:, :, 0:D].rearrange("p c (h e) -> p c h e", e=E1), over(rden, E1), ALU.mult).then_inc(S["o1"], 1)

            def add_linear(t):
                xc = x[:, bass.ds(t * NC, NC), :]
                dve.wait_ge(S["y1_ps"], t + 1)
                lt(t, V.tensor_tensor(prod[:, :, :], tb[:, 0, :].rearrange(nat, c=NC), every(bo, NC), ALU.add))
                lt(t, V.tensor_tensor(xc, xc, prod[:, :, :], ALU.add))

            def token_scores(t):
                dve.wait_ge(S["xn_t"], NC * (2 * t + 2))
                lt(t, V.tensor_tensor(prod[:, :, :], xn_t[:, :, :], every(wrt, NC), ALU.mult))
                V.tensor_reduce(score[:, :], prod[:, :, :], AX.X, ALU.add).then_inc(S["score_col"], 1)

            def token_ranks(t, c):
                dve.wait_ge(S["score_ps"], t + 1)
                V.tensor_scalar(scr[:, 0, c, :], tb[:, 1, :], score[:, c:c + 1], None, ALU.is_gt, ALU.add, accum_out=above[:, 0, c:c + 1])
                ins = V.scalar_tensor_tensor(scr[:, 1, c, :], tb[:, 1, :], score[:, c:c + 1],
                                             ttri[:, (NC - 1 - c) * P:(2 * NC - 1 - c) * P], ALU.is_equal, ALU.mult,
                                             accum_out=above[:, 1, c:c + 1])
                if c == NC - 1:
                    lt(t, ins)

            def kept(t):
                lt(t, V.tensor_tensor(above[:, 0, :], above[:, 0, :], above[:, 1, :], ALU.add))
                V.tensor_scalar(keep[:, 0, :], above[:, 0, :], float(KEEP), None, ALU.is_lt)
                lt(t, V.tensor_scalar(keep[:, 1, :], above[:, 0, :], float(KEEP), None, ALU.is_ge))

            def result_others(t):
                dve.wait_ge(S["out_dma"], 16 * t + 1)
                for c in range(NC):
                    ins = V.scalar_tensor_tensor(res[:, c, :], xn_t[:, c, :], keep[:, 1, c:c + 1], chunk(x, t, c), ALU.mult, ALU.add)
                lt(t, ins)

            def result_kept(t):
                dve.wait_ge(S["gel"], t + 1)
                for c in range(NC):
                    ins = V.scalar_tensor_tensor(res[:, c, :], gel[:, c, :], keep[:, 0, c:c + 1], res[:, c, :], ALU.mult, ALU.add)
                ins.then_inc(S["res"], 1)

            def split_w1(e):
                dve.wait_ge(in_w1[e], 16)
                V.tensor_copy(w1s[0][:, e, :], w1[:, e, :]).then_inc(S["w1s"], 1)
                dve.wait_ge(S["w1s"], 2 * e + 1)
                V.tensor_tensor(w1s[1][:, e, :], w1[:, e, :], w1s[0][:, e, :].bitcast(F32), ALU.subtract).then_inc(S["w1s"], 1)

            def finish(t, k):
                if k < NC:
                    token_ranks(t, k)
                else:
                    kept(t)
                    result_others(t)
                    result_kept(t)

            def batch(b, finishes=True, tail=True, front=True):
                t, f = b - 1, b + 1
                for k in range(NU):
                    if finishes and k <= NC:
                        finish(t - 1, k)
                    if not front and k >= NU - 3:
                        finish(t, k - (NU - 3))
                    if tail:
                        if k == 5:
                            add_experts(t)
                            tail_stats(t, 0)
                        if k == 7:
                            tail_norm(t, 0)
                        if k == 12:
                            add_kv_bias(t)
                        if k == 13:
                            decayed_keys(t)
                        if k == 16:
                            mask_heads(t)
                        if k == 18:
                            denominators(t)
                            divide(t)
                        if k == 22:
                            add_linear(t)
                            tail_stats(t, 1)
                        if k == 24:
                            tail_norm(t, 1)
                        if k == 25:
                            token_scores(t)
                    if front:
                        if k == 8:
                            front_stats(f)
                        if k == 10:
                            front_norm(f)
                        if k == 16:
                            softmax_start(f)
                        if k == 18:
                            softmax_end(f)
                        if k == 19:
                            expert_ranks(f)
                        if k == 20:
                            routing(f)
                        if k == 31:
                            dve.wait_ge(S["z"], b * NU + NU)
                            hand_over(f)
                    if isinstance(b, int) and b == 0 and k % NF == 1 and k // NF + 2 < NE:
                        split_w1(k // NF + 2)
                    if isinstance(b, int) and b == 0 and k == 2:
                        dve.wait_ge(S["in_rest_x"], 16)
                    n = b * NU + k
                    if k % NF == 0:
                        dve.wait_ge(S["rb"], b * NE + k // NF + 1)
                    dve.wait_ge(S["hr"], n + 1)
                    if not isinstance(n, int) or n >= 4:
                        dve.wait_ge(S["hml"], n - 3)
                    V.tensor_tensor(hm[:, k % 4, :], hr[:, k % 2, :], rb[:, (k // NF) % 2, :], ALU.mult).then_inc(S["hm"], 1)

            dve.wait_ge(S["in_x"], 16)
            front_stats(0)
            front_norm(0)
            split_w1(0)
            dve.wait_ge(S["in_front"], 16 * len(front_loads))
            softmax_start(0)
            softmax_end(0)
            expert_ranks(0)
            routing(0)
            hand_over(0)
            split_w1(1)
            batch(0, finishes=False, tail=False)
            dve.wait_ge(S["in_tail"], 16 * len(tail_loads))
            dve.wait_ge(S["ones2"], 1)
            batch(1, finishes=False)
            with dve.Fori(2, B - 1) as b:
                batch(b)
            batch(B - 1, front=False)
            t = B - 1
            for k in range(3, NC + 1):
                finish(t - 1, k)
            add_experts(t)
            tail_stats(t, 0)
            tail_norm(t, 0)
            add_kv_bias(t)
            decayed_keys(t)
            mask_heads(t)
            denominators(t)
            divide(t)
            add_linear(t)
            tail_stats(t, 1)
            tail_norm(t, 1)
            token_scores(t)
            for k in range(NC + 1):
                finish(t, k)


def constants():
    f = np.float32
    nsel = np.zeros((P, 2, P), f)
    for i in range(2):
        for v in range(2):
            nsel[64 * v:64 * v + 64, i, 64 * i + 32 * v] = 1
    head = np.arange(D) // E1
    hmask = np.concatenate([head[:, None] == head[None, :], head[:, None] == np.arange(H1)[None, :]], 1).astype(f)
    e = np.arange(NE)
    etri = np.broadcast_to((e[None, :] < e[:, None]).astype(f), (P, NE, NE)).copy()
    j = np.arange((2 * NC - 1) * P) - (NC - 1) * P
    ttri = (j[None, :] < np.arange(P)[:, None]).astype(f)
    dec = np.exp(-np.arange(T, dtype=f) / f(T)).astype(f).reshape(NC, P).T.copy()
    return {"c_ident": np.eye(P, dtype=f), "c_nsel": nsel, "c_hmask": hmask, "c_etri": etri, "c_ttri": ttri, "c_dec": dec}


def kernel(**inputs):
    import concourse.bacc as _bacc
    from concourse.bass_utils import run_bass_kernel_spmd as _run

    i = {k: np.ascontiguousarray(v) for k, v in inputs.items()}
    win = i["L0_attn_W_in"].reshape(D, PAIRS, 2, 4, E0)
    bin_ = i["L0_attn_b_in"].reshape(PAIRS, 2, 4, E0)
    arrays = {
        "X": i["L0_attn_X"].reshape(B * T, D),
        "W_qkg": win[:, :, :, [0, 1, 3]].transpose(0, 1, 3, 2, 4).reshape(D, PAIRS, 3, P),
        "b_qkg": bin_[:, :, [0, 1, 3]].transpose(1, 3, 0, 2).reshape(P, PAIRS, 3),
        "W_v": win[:, :, :, 2].reshape(D, H0 * E0),
        "b_v": bin_[:, :, 2].reshape(H0 * E0),
        "W_out": i["L0_attn_W_out"], "b_out": i["L0_attn_b_out"],
        "W1": i["L0_ffn_W1"], "b1": i["L0_ffn_b1"].reshape(NE * NF, P).T,
        "W2": i["L0_ffn_W2"], "b2": i["L0_ffn_b2"], "Wr": i["L0_ffn_Wr"], "br": i["L0_ffn_br"],
        "W_q": i["L1_attn_W_q"].T, "b_q": i["L1_attn_b_q"],
        "W_kv": np.concatenate([i["L1_attn_W_k"].T, i["L1_attn_W_v"].T], 1),
        "b_kv": np.concatenate([i["L1_attn_b_k"], i["L1_attn_b_v"]]),
        "W_o": i["L1_attn_W_o"].T, "b_o": i["L1_attn_b_o"],
        "w_router": i["L1_ffn_w_router"], "w_block": i["L1_ffn_w_block"],
        **constants(),
    }
    arrays = {k: np.ascontiguousarray(v) for k, v in arrays.items()}
    nc = _bacc.Bacc("TRN2", target_bir_lowering=False, num_devices=1)
    a = {k: nc.dram_tensor(f"in_{k}", v.shape, F32, kind="ExternalInput").ap() for k, v in arrays.items()}
    out = nc.dram_tensor("out", (B, T, D), F32, kind="ExternalOutput").ap()
    build(nc, a, out)
    r = _run(nc, [{f"in_{k}": v for k, v in arrays.items()}], core_ids=[0])
    return r.results[0]["out"]
```
